# Optimizing a Trainium2 kernel written in Bass

```python
import numpy as np
import jax
import jax.numpy as jnp

def _softmax(x, axis=-1):
    return jax.nn.softmax(x, axis=axis)

def _gelu(x):
    return jax.nn.gelu(x, approximate=True)

def _silu(x):
    return jax.nn.silu(x)

def _sigmoid(x):
    return jax.nn.sigmoid(x)

def _layernorm(x, axis=-1, eps=1e-05):
    m = jnp.mean(x, axis=axis, keepdims=True)
    v = jnp.var(x, axis=axis, keepdims=True)
    return (x - m) / jnp.sqrt(v + eps)

def _scatter_add(tgt, idx, src, axis=0):
    return tgt.at[idx].add(src)

def _segment_sum(src, seg, n):
    return jax.ops.segment_sum(src, seg, n)
kernel_name = 'mk_pixart_seq_d1_seqx_r4_915f68'

def setup_inputs(seed: int=0):
    np.random.seed(seed)
    _w = jnp.asarray

    def _rec_inputs():
        import jax
        import jax.numpy as jnp
        _rk = jax.random.key(seed)
        x = -0.0005207 + 1.001 * jax.random.normal(jax.random.fold_in(_rk, 1), (4, 512, 256), jnp.float32)
        _lenS = 512 - jax.random.randint(jax.random.fold_in(_rk, 7), (4,), 0, max(1, 512 // 4) + 1, jnp.int32)
        _lenS2 = 512 - jax.random.randint(jax.random.fold_in(_rk, 8), (4,), 0, max(1, 512 // 4) + 1, jnp.int32)
        cond_1024 = 0.000887014 + 1.03683 * jax.random.normal(jax.random.fold_in(_rk, 11), (4, 256), jnp.float32)
        _ctx_768P = jax.random.normal(jax.random.fold_in(_rk, 12), (4, 16, 192), jnp.float32)
        _ctx_768c = jax.random.dirichlet(jax.random.fold_in(_rk, 512), 0.3 * jnp.ones((16,), jnp.float32), (4, 512))
        _ctx_768t = jnp.einsum('bsk,bkd->bsd', _ctx_768c, _ctx_768P)
        _ctx_768t = _ctx_768t * jax.lax.rsqrt(jnp.mean(jnp.square(_ctx_768t)) + 1e-12) * 0.953939
        ctx_768 = 0.000599585 + 1.00006 * (_ctx_768t + 0.3 * jax.random.normal(jax.random.fold_in(_rk, 612), (4, 512, 192), jnp.float32))
        return (x, cond_1024, ctx_768)
    x, cond_1024, ctx_768 = _rec_inputs()

    def _L0_xcond_setup():
        import jax, jax.numpy as jnp
        import numpy as np
        B, N, M = (2, 256, 128)
        D, H, DH = (256, 16, 64)
        MID = H * DH
        DC = 192
        MULT = 4
        EPS = 1e-05

        def _ln(x, w, b):
            mu = jnp.mean(x, -1, keepdims=True)
            var = jnp.mean((x - mu) ** 2, -1, keepdims=True)
            return (x - mu) * jax.lax.rsqrt(var + EPS) * w + b

        def _sincos(n, d):
            inv = 1.0 / 10000.0 ** (jnp.arange(0, d, 2, dtype=jnp.float32) / d)
            ang = jnp.arange(n, dtype=jnp.float32)[:, None] * inv[None, :]
            return (jnp.sin(ang), jnp.cos(ang))

        def _rope(x, sin, cos):
            s = sin[None, None]
            c = cos[None, None]
            xe = x[..., ::2]
            xo = x[..., 1::2]
            re = xe * c - xo * s
            ro = xe * s + xo * c
            return jnp.stack((re, ro), axis=-1).reshape(x.shape)

        def _heads(t):
            b, n, _ = t.shape
            return t.reshape(b, n, H, DH).transpose(0, 2, 1, 3)

        def _attn(xq, ctx, wq, wkv, wo, bo):
            q = _heads(xq @ wq)
            k, v = jnp.split(ctx @ wkv, 2, axis=-1)
            k = _heads(k)
            v = _heads(v)
            sq, cq = _sincos(q.shape[2], DH)
            sk, ck = _sincos(k.shape[2], DH)
            q = _rope(q, sq, cq)
            k = _rope(k, sk, ck)
            sim = jnp.einsum('bhnd,bhmd->bhnm', q, k) * DH ** (-0.5)
            a = jax.nn.softmax(sim, axis=-1)
            o = jnp.einsum('bhnm,bhmd->bhnd', a, v)
            o = o.transpose(0, 2, 1, 3).reshape(xq.shape[0], xq.shape[1], MID)
            return o @ wo + bo

        def _adaln(x, c, lw, lb, gw, gb, bw, bb):
            g = (c @ gw + gb)[:, None, :]
            bt = (c @ bw + bb)[:, None, :]
            return _ln(x, lw, lb) * (1.0 + g) + bt
        ks = jax.random.split(jax.random.key(seed), 24)
        s = 0.02
        inp = {'x': jax.random.normal(ks[0], (B, N, D), jnp.float32), 'cond': jax.random.normal(ks[1], (B, D), jnp.float32), 'context': jax.random.normal(ks[2], (B, M, DC), jnp.float32), 'ln1_w': jnp.ones((D,), jnp.float32), 'ln1_b': jnp.zeros((D,), jnp.float32), 'g1_w': jax.random.normal(ks[3], (D, D), jnp.float32) * s, 'g1_b': jnp.zeros((D,), jnp.float32), 'b1_w': jax.random.normal(ks[4], (D, D), jnp.float32) * s, 'b1_b': jnp.zeros((D,), jnp.float32), 'ln2_w': jnp.ones((D,), jnp.float32), 'ln2_b': jnp.zeros((D,), jnp.float32), 'g2_w': jax.random.normal(ks[5], (D, D), jnp.float32) * s, 'g2_b': jnp.zeros((D,), jnp.float32), 'b2_w': jax.random.normal(ks[6], (D, D), jnp.float32) * s, 'b2_b': jnp.zeros((D,), jnp.float32), 'sa_wq': jax.random.normal(ks[7], (D, MID), jnp.float32) * s, 'sa_wkv': jax.random.normal(ks[8], (D, 2 * MID), jnp.float32) * s, 'sa_wo': jax.random.normal(ks[9], (MID, D), jnp.float32) * s, 'sa_bo': jnp.zeros((D,), jnp.float32), 'ca_lnc_w': jnp.ones((DC,), jnp.float32), 'ca_lnc_b': jnp.zeros((DC,), jnp.float32), 'ca_wq': jax.random.normal(ks[10], (D, MID), jnp.float32) * s, 'ca_wkv': jax.random.normal(ks[11], (DC, 2 * MID), jnp.float32) * s, 'ca_wo': jax.random.normal(ks[12], (MID, D), jnp.float32) * s, 'ca_bo': jnp.zeros((D,), jnp.float32), 'ff_w1': jax.random.normal(ks[13], (D, MULT * D), jnp.float32) * s, 'ff_b1': jnp.zeros((MULT * D,), jnp.float32), 'ff_w2': jax.random.normal(ks[14], (MULT * D, D), jnp.float32) * s, 'ff_b2': jnp.zeros((D,), jnp.float32)}
        return inp
    _L0_xcond_all = _L0_xcond_setup()
    _L0_xcond_in = {k: v for k, v in _L0_xcond_all.items() if k in ('ln1_w', 'ln1_b', 'g1_w', 'g1_b', 'b1_w', 'b1_b', 'ln2_w', 'ln2_b', 'g2_w', 'g2_b', 'b2_w', 'b2_b', 'sa_wq', 'sa_wkv', 'sa_wo', 'sa_bo', 'ca_lnc_w', 'ca_lnc_b', 'ca_wq', 'ca_wkv', 'ca_wo', 'ca_bo', 'ff_w1', 'ff_b1', 'ff_w2', 'ff_b2')}
    del _L0_xcond_all
    return {'x': x, 'cond_1024': cond_1024, 'ctx_768': ctx_768, 'L0_xcond_ln1_w': _L0_xcond_in['ln1_w'], 'L0_xcond_ln1_b': _L0_xcond_in['ln1_b'], 'L0_xcond_g1_w': _L0_xcond_in['g1_w'], 'L0_xcond_g1_b': _L0_xcond_in['g1_b'], 'L0_xcond_b1_w': _L0_xcond_in['b1_w'], 'L0_xcond_b1_b': _L0_xcond_in['b1_b'], 'L0_xcond_ln2_w': _L0_xcond_in['ln2_w'], 'L0_xcond_ln2_b': _L0_xcond_in['ln2_b'], 'L0_xcond_g2_w': _L0_xcond_in['g2_w'], 'L0_xcond_g2_b': _L0_xcond_in['g2_b'], 'L0_xcond_b2_w': _L0_xcond_in['b2_w'], 'L0_xcond_b2_b': _L0_xcond_in['b2_b'], 'L0_xcond_sa_wq': _L0_xcond_in['sa_wq'], 'L0_xcond_sa_wkv': _L0_xcond_in['sa_wkv'], 'L0_xcond_sa_wo': _L0_xcond_in['sa_wo'], 'L0_xcond_sa_bo': _L0_xcond_in['sa_bo'], 'L0_xcond_ca_lnc_w': _L0_xcond_in['ca_lnc_w'], 'L0_xcond_ca_lnc_b': _L0_xcond_in['ca_lnc_b'], 'L0_xcond_ca_wq': _L0_xcond_in['ca_wq'], 'L0_xcond_ca_wkv': _L0_xcond_in['ca_wkv'], 'L0_xcond_ca_wo': _L0_xcond_in['ca_wo'], 'L0_xcond_ca_bo': _L0_xcond_in['ca_bo'], 'L0_xcond_ff_w1': _L0_xcond_in['ff_w1'], 'L0_xcond_ff_b1': _L0_xcond_in['ff_b1'], 'L0_xcond_ff_w2': _L0_xcond_in['ff_w2'], 'L0_xcond_ff_b2': _L0_xcond_in['ff_b2']}

def reference(x, cond_1024, ctx_768, L0_xcond_ln1_w, L0_xcond_ln1_b, L0_xcond_g1_w, L0_xcond_g1_b, L0_xcond_b1_w, L0_xcond_b1_b, L0_xcond_ln2_w, L0_xcond_ln2_b, L0_xcond_g2_w, L0_xcond_g2_b, L0_xcond_b2_w, L0_xcond_b2_b, L0_xcond_sa_wq, L0_xcond_sa_wkv, L0_xcond_sa_wo, L0_xcond_sa_bo, L0_xcond_ca_lnc_w, L0_xcond_ca_lnc_b, L0_xcond_ca_wq, L0_xcond_ca_wkv, L0_xcond_ca_wo, L0_xcond_ca_bo, L0_xcond_ff_w1, L0_xcond_ff_b1, L0_xcond_ff_w2, L0_xcond_ff_b2):
    import jax
    import jax.numpy as jnp

    def _L0_xcond_ref(x, cond, context, ln1_w, ln1_b, g1_w, g1_b, b1_w, b1_b, ln2_w, ln2_b, g2_w, g2_b, b2_w, b2_b, sa_wq, sa_wkv, sa_wo, sa_bo, ca_lnc_w, ca_lnc_b, ca_wq, ca_wkv, ca_wo, ca_bo, ff_w1, ff_b1, ff_w2, ff_b2):
        import jax, jax.numpy as jnp
        import numpy as np
        B, N, M = (2, 256, 128)
        D, H, DH = (256, 16, 64)
        MID = H * DH
        DC = 192
        MULT = 4
        EPS = 1e-05

        def _ln(x, w, b):
            mu = jnp.mean(x, -1, keepdims=True)
            var = jnp.mean((x - mu) ** 2, -1, keepdims=True)
            return (x - mu) * jax.lax.rsqrt(var + EPS) * w + b

        def _sincos(n, d):
            inv = 1.0 / 10000.0 ** (jnp.arange(0, d, 2, dtype=jnp.float32) / d)
            ang = jnp.arange(n, dtype=jnp.float32)[:, None] * inv[None, :]
            return (jnp.sin(ang), jnp.cos(ang))

        def _rope(x, sin, cos):
            s = sin[None, None]
            c = cos[None, None]
            xe = x[..., ::2]
            xo = x[..., 1::2]
            re = xe * c - xo * s
            ro = xe * s + xo * c
            return jnp.stack((re, ro), axis=-1).reshape(x.shape)

        def _heads(t):
            b, n, _ = t.shape
            return t.reshape(b, n, H, DH).transpose(0, 2, 1, 3)

        def _attn(xq, ctx, wq, wkv, wo, bo):
            q = _heads(xq @ wq)
            k, v = jnp.split(ctx @ wkv, 2, axis=-1)
            k = _heads(k)
            v = _heads(v)
            sq, cq = _sincos(q.shape[2], DH)
            sk, ck = _sincos(k.shape[2], DH)
            q = _rope(q, sq, cq)
            k = _rope(k, sk, ck)
            sim = jnp.einsum('bhnd,bhmd->bhnm', q, k) * DH ** (-0.5)
            a = jax.nn.softmax(sim, axis=-1)
            o = jnp.einsum('bhnm,bhmd->bhnd', a, v)
            o = o.transpose(0, 2, 1, 3).reshape(xq.shape[0], xq.shape[1], MID)
            return o @ wo + bo

        def _adaln(x, c, lw, lb, gw, gb, bw, bb):
            g = (c @ gw + gb)[:, None, :]
            bt = (c @ bw + bb)[:, None, :]
            return _ln(x, lw, lb) * (1.0 + g) + bt
        attn_in = _adaln(x, cond, ln1_w, ln1_b, g1_w, g1_b, b1_w, b1_b)
        x = _attn(attn_in, attn_in, sa_wq, sa_wkv, sa_wo, sa_bo) + x
        cross_in = _adaln(x, cond, ln1_w, ln1_b, g1_w, g1_b, b1_w, b1_b)
        ctx_n = _ln(context, ca_lnc_w, ca_lnc_b)
        x = _attn(cross_in, ctx_n, ca_wq, ca_wkv, ca_wo, ca_bo) + x
        ffn_in = _adaln(x, cond, ln2_w, ln2_b, g2_w, g2_b, b2_w, b2_b)
        h = jax.nn.gelu(ffn_in @ ff_w1 + ff_b1, approximate=False)
        x = h @ ff_w2 + ff_b2 + x
        return x
    x = _L0_xcond_ref(x, cond_1024, ctx_768, L0_xcond_ln1_w, L0_xcond_ln1_b, L0_xcond_g1_w, L0_xcond_g1_b, L0_xcond_b1_w, L0_xcond_b1_b, L0_xcond_ln2_w, L0_xcond_ln2_b, L0_xcond_g2_w, L0_xcond_g2_b, L0_xcond_b2_w, L0_xcond_b2_b, L0_xcond_sa_wq, L0_xcond_sa_wkv, L0_xcond_sa_wo, L0_xcond_sa_bo, L0_xcond_ca_lnc_w, L0_xcond_ca_lnc_b, L0_xcond_ca_wq, L0_xcond_ca_wkv, L0_xcond_ca_wo, L0_xcond_ca_bo, L0_xcond_ff_w1, L0_xcond_ff_b1, L0_xcond_ff_w2, L0_xcond_ff_b2)
    return x

_drawn_inputs = setup_inputs


def setup_inputs(seed=0):
    import zlib

    import numpy as np

    out = dict(_drawn_inputs(seed))
    spreads = {'L0_xcond_ln1_w': (1.0, 0.6),
     'L0_xcond_ln1_b': (0.0, 0.384),
     'L0_xcond_g1_b': (0.0, 0.8),
     'L0_xcond_b1_b': (0.0, 0.358),
     'L0_xcond_ln2_w': (1.0, 0.6),
     'L0_xcond_ln2_b': (0.0, 0.618),
     'L0_xcond_g2_b': (0.0, 0.693),
     'L0_xcond_b2_b': (0.0, 0.764),
     'L0_xcond_sa_bo': (0.0, 0.1),
     'L0_xcond_ca_lnc_w': (1.0, 0.6),
     'L0_xcond_ca_lnc_b': (0.0, 0.531),
     'L0_xcond_ca_bo': (0.0, 0.1),
     'L0_xcond_ff_b1': (0.0, 0.271),
     'L0_xcond_ff_b2': (0.0, 0.1)}
    factors = {'L0_xcond_g1_w': 7.83, 'L0_xcond_sa_wq': 8.0, 'L0_xcond_ca_wq': 8.0}
    for name, (base, spread) in spreads.items():
        noise = np.random.default_rng([zlib.crc32(name.encode()), seed]).standard_normal(out[name].shape)
        drawn = base * np.exp(spread * noise) if base else spread * noise
        out[name] = jnp.asarray(drawn.astype(out[name].dtype))
    for name, factor in factors.items():
        out[name] = (out[name] * factor).astype(out[name].dtype)
    return out
```

```python
import concourse.bass as bass
from concourse import mybir
from contextlib import ExitStack

F32 = mybir.dt.float32
F32R = mybir.dt.float32r
I32 = mybir.dt.int32
ALU = mybir.AluOpType
ACT = mybir.ActivationFunctionType
AX = mybir.AxisListType

NB = 4
N = 512
TT = N // 128
D = 256
KT = D // 128
DC = 192
CK = DC // KT
DH = 64
H = 16
NP = H // 2
FF = 4 * D
FT = FF // 128
EPS = 1e-5
NEWTON = 3
RSQRT_GUESS = float(0x5F3759DF)
QKV = 3 * 128
WQKV = KT * QKV
WPACK = WQKV + D
T_BLOCKS = 2 * TT
S_TILES = 2 * TT
X_ROUNDS = 4
CROSS = NP


def build(nc, x_d, ctx_d, pack_d, cond_d, ada_d, cols_d, ctxln_d, rows_d, w1_d, w2_d, rope_d, out_d):
    stack = ExitStack()
    with stack:
        attention_only = ExitStack()

        def sb(name, shape, dt=F32, where=stack):
            return where.enter_context(nc.sbuf_tensor(name, shape, dt))

        def sem(name):
            return stack.enter_context(nc.semaphore(name))

        x = sb("x", [128, NB, TT, D])
        xn_hi = sb("xn_hi", [128, NB, KT, N], F32R)
        xn_lo = sb("xn_lo", [128, NB, KT, N], F32R)
        ident = sb("ident", [128, 128])
        zero = sb("zero", [128, 1])
        cols = sb("cols", [128, 8 * KT + FT])
        cond = sb("cond", [128, KT, NB])
        ada_scale = sb("ada_scale", [128, 2, KT, NB])
        ada_shift = sb("ada_shift", [128, 2, KT, NB])
        ada_g1 = sb("ada_g1", [128, 2, KT, NB])
        ada_gb = sb("ada_gb", [128, 2, KT, NB])
        bias_rows = sb("bias_rows", [128, 3, D])
        stats = sb("stats", [128, TT, 6])
        mean_var = sb("mean_var", [128, TT, 2])
        rstd = sb("rstd", [128, TT])
        var_eps = sb("var_eps", [128, TT])
        newton = sb("newton", [128, TT])
        z = sb("z", [128, TT, D])
        y = sb("y", [128, N])

        def asb(name, shape, dt=F32):
            return sb(name, shape, dt, attention_only)

        ctx_hi = asb("ctx_hi", [128, NB, KT, N], F32R)
        ctx_lo = asb("ctx_lo", [128, NB, KT, N], F32R)
        ctx_in = asb("ctx_rows", [128, NB, TT, DC])
        ctx_ln = asb("ctx_ln", [CK, 2, KT])
        ada_w = asb("ada_w", [128, 4, KT, D])
        rope = asb("rope", [128, 2, TT, 4, DH])
        w_raw = asb("w_raw", [128, WPACK])
        w_hi = asb("w_hi", [128, WQKV], F32R)
        w_lo = asb("w_lo", [128, WQKV], F32R)
        wo_hi = asb("wo_hi", [128, D], F32R)
        wo_lo = asb("wo_lo", [128, D], F32R)
        rot_a = asb("rot_a", [128, 2, 4, DH])
        rot_b = asb("rot_b", [128, 2, 4, DH])
        rotated = asb("rotated", [128, TT, 4, 2, DH])
        q_hi = asb("q_hi", [128, 2, 2, N], F32R)
        q_lo = asb("q_lo", [128, 2, 2, N], F32R)
        k_parts = asb("k_parts", [128, 2, 2, N], F32R)
        v = asb("v", [128, 2, TT, 128])
        probs = asb("probs", [128, S_TILES, N])
        probs_t = asb("probs_t", [128, T_BLOCKS, N])
        neg_max = asb("neg_max", [128, 2, S_TILES])
        row_sum = asb("row_sum", [128, 2, S_TILES])
        row_inv = asb("row_inv", [128, 2, S_TILES])
        o_hi = asb("o_hi", [128, N], F32R)
        o_lo = asb("o_lo", [128, N], F32R)
        attention_only.close()

        w1_hi = sb("w1_hi", [128, KT, FF], F32R)
        w1_lo = sb("w1_lo", [128, KT, FF], F32R)
        w2_hi = sb("w2_hi", [128, FT, D], F32R)
        w2_lo = sb("w2_lo", [128, FT, D], F32R)
        w1_raw = sb("w1_raw", [128, KT, FF])
        w2_raw = sb("w2_raw", [128, FT, D])
        hid = sb("hid", [128, 4, N])
        hid_hi = sb("hid_hi", [128, 4, N], F32R)
        hid_lo = sb("hid_lo", [128, 4, N], F32R)

        ps = stack.enter_context(nc.psum_tensor("ps", [128, 8, N], F32))
        score_ps = (ps[:, 0, :], ps[:, 1, :])
        turn_ps = (ps[:, 2, :], ps[:, 3, :])
        av_ps = ps[:, 4, :]
        proj_ps = ps[:, 5, :]
        side_ps = ps[:, 6, :]
        out_ps = ps[:, 7, :]

        ada_in = sem("ada_in")
        cols_in = sem("cols_in")
        rope_in = sem("rope_in")
        rows_in = sem("rows_in")
        x_in = [sem(f"x_in{b}") for b in range(NB)]
        ctx_loaded = sem("ctx_loaded")
        ident_ready = sem("ident_ready")
        zero_ready = sem("zero_ready")
        ada_mm = sem("ada_mm")
        ada_step = sem("ada_step")
        ln_step = sem("ln_step")
        ln_turned = sem("ln_turned")
        ln_scaled = sem("ln_scaled")
        ln_rounded = sem("ln_rounded")
        ln_split = sem("ln_split")
        biased = sem("biased")
        w_loaded = sem("w_loaded")
        w_step = sem("w_step")
        w_split = sem("w_split")
        wo_step = sem("wo_step")
        wo_split = sem("wo_split")
        projected = sem("projected")
        roped = sem("roped")
        v_ready = sem("v_ready")
        rot_ready = sem("rot_ready")
        qk_turned = sem("qk_turned")
        qk_high = sem("qk_high")
        qk_low = sem("qk_low")
        scored = sem("scored")
        maxed = sem("maxed")
        exped = sem("exped")
        inverted = sem("inverted")
        normed = sem("normed")
        turned = sem("turned")
        probs_t_ready = sem("probs_t_ready")
        averaged = sem("averaged")
        o_high = sem("o_high")
        o_low = sem("o_low")
        o_projected = sem("o_projected")
        o_added = sem("o_added")
        ffw_loaded = sem("ffw_loaded")
        ffw_high = sem("ffw_high")
        ffw_split = sem("ffw_split")
        hid_mm = sem("hid_mm")
        hid_ready = sem("hid_ready")
        hid_rounded = sem("hid_rounded")
        hid_split = sem("hid_split")
        y_step = sem("y_step")
        y_added = sem("y_added")
        stored = sem("stored")

        X, C = 0, 1
        order = [(X, b, 0) for b in range(NB)]
        after_self = {0: [(C, 0)], 1: [(C, 1), (X, 0)], 2: [(C, 2), (X, 1)], 3: [(C, 3), (X, 2)], 4: [(X, 3)]}
        after_cross = {1: [(X, 0)], 2: [(X, 1)], 3: [(X, 2)], 4: [(X, 3)]}
        for slots, ada in ((after_self, 0), (after_cross, 1)):
            for s in sorted(slots):
                order += [(kind, b, ada) for kind, b in slots[s]]
        place = {}
        for n, (kind, b, ada) in enumerate(order):
            place[(kind, b, len([1 for o in order[:n] if o[0] == kind and o[1] == b]))] = n

        def norms(phase, s):
            which = (after_self, after_cross)[phase].get(s, [])
            return [place[(kind, b, (phase + 1) if kind == X else 0)] for kind, b in which]

        def x_norms_before(n):
            return sum(1 for kind, _, _ in order[:n] if kind == X)

        UNITS = 4 * 2 * NP
        X_READ = 3 * TT + 2 + 3 * NEWTON

        def run_slots(eng, slot, norm):
            done = NB
            for phase in range(2):
                first = phase * NP
                with eng.Fori(first, first + NP - 1) as w:
                    for b in range(NB):
                        slot(w * 4 + b, b, w, phase, phase, [], done)
                w = first + NP - 1
                for b in range(NB):
                    after = phase if b < NB - 1 else phase + 1
                    lns = norms(phase, b)
                    slot(4 * w + b, b, w, phase, after if after < 2 else None, lns, done)
                    done += len(lns)
                for n in norms(phase, NB):
                    norm(n)
                    done += 1

        def source(n):
            kind, b, _ = order[n]
            return (x[:, b, :, :], 128) if kind == X else (ctx_in[:, b, :, :], CK)

        ADA_STEPS = 4 * 2 * KT
        block = stack.enter_context(nc.Block())

        @block.sync
        def _(sp):
            sp.dma_start(x[:, 0, :, :], x_d[0].rearrange("(t p) d -> p t d", p=128)).then_inc(x_in[0], 16)
            sp.dma_start(w_raw[:, :], pack_d[0]).then_inc(w_loaded, 16)
            for b in range(1, NB):
                sp.dma_start(x[:, b, :, :], x_d[b].rearrange("(t p) d -> p t d", p=128)).then_inc(x_in[b], 16)
            for b in range(NB):
                sp.dma_start(ctx_in[:, b, :, :], ctx_d[b].rearrange("(t p) d -> p t d", p=128))\
                  .then_inc(ctx_loaded, 16)
            with sp.Fori(1, 2 * NP) as w:
                sp.wait_ge(wo_split, w)
                sp.dma_start(w_raw[:, :], pack_d[bass.ds(w, 1), :, :].rearrange("a p c -> p (a c)"))\
                  .then_inc(w_loaded, 16)
            sp.wait_ge(ln_split, 2 * place[(C, NB - 1, 0)] + 2)
            sp.dma_start(w1_raw[:, :, :], w1_d).then_inc(ffw_loaded, 16)
            sp.dma_start(w2_raw[:, :, :], w2_d).then_inc(ffw_loaded, 16)
            with sp.Fori(0, NB) as b:
                sp.wait_ge(y_added, b + 1)
                sp.dma_start(out_d[bass.ds(b, 1), :, :].rearrange("a (t p) d -> p (a t) d", p=128),
                             x[:, bass.ds(b, 1), :, :].rearrange("p a t d -> p (a t) d")).then_inc(stored, 16)
            sp.wait_ge(stored, 16 * NB)

        @block.gpsimd
        def _(pool):
            pool.memset(ident[:, :], 0.0).then_inc(ident_ready, 1)
            pool.memset(zero[:, :], 0.0).then_inc(zero_ready, 1)
            pool.wait_ge(ident_ready, 1)
            pool.affine_select(out=ident[:, :], in_=ident[:, :], compare_op=ALU.not_equal, fill=1.0,
                               base=0, pattern=[[-1, 128]], channel_multiplier=1).then_inc(ident_ready, 1)

            def split_w(w):
                pool.wait_ge(w_loaded, 16 * w + 16)
                raw = w_raw[:, 0:WQKV]
                pool.tensor_tensor(w_hi[:, :], raw, zero[:, :].broadcast_to([128, WQKV]), ALU.add).then_inc(w_step, 1)
                pool.wait_ge(w_step, w + 1)
                pool.tensor_tensor(w_lo[:, :], raw, w_hi[:, :], ALU.subtract).then_inc(w_split, 1)

            def split_wo(w):
                raw = w_raw[:, WQKV:WPACK]
                pool.tensor_tensor(wo_hi[:, :], raw, zero[:, :].broadcast_to([128, D]), ALU.add).then_inc(wo_step, 1)
                pool.wait_ge(wo_step, w + 1)
                pool.tensor_tensor(wo_lo[:, :], raw, wo_hi[:, :], ALU.subtract)\
                    .then_inc(wo_split, 1)

            def add_rotation(u, tt):
                pool.wait_ge(roped, 4 * u + tt + 1)
                a = rot_a[:, tt % 2, :, :].unsqueeze(2).broadcast_to([128, 4, 2, DH])
                c = rot_b[:, tt % 2, :, :].unsqueeze(2).broadcast_to([128, 4, 2, DH])
                pool.tensor_tensor(rotated[:, tt, :, :, :], a, c, ALU.add).then_inc(rot_ready, 1)

            def add_bias(n):
                kind, b, _ = order[n]
                if kind == X:
                    k = sum(1 for kind, _, _ in order[:n] if kind == X) // NB
                    pool.wait_ge(ln_step, X_READ * (n + 1))
                    pool.tensor_tensor(x[:, b, :, :], x[:, b, :, :],
                                       bias_rows[:, k, :].unsqueeze(1).broadcast_to([128, TT, D]),
                                       ALU.add).then_inc(biased, 1)

            pool.wait_ge(zero_ready, 1)
            split_w(0)
            for tt in range(TT):
                add_rotation(0, tt)
            pool.wait_ge(rows_in, 16)
            for n in range(NB):
                add_bias(n)

            def slot(u, b, w, phase, after, lns, done):
                if after is not None:
                    for tt in range(TT):
                        if tt == 0:
                            pool.wait_ge(qk_turned, 4 * u + 4)
                        add_rotation(u + 1, tt)
                        if tt == 0 and b == 0:
                            split_wo(w)
                if b == 2 and not (isinstance(w, int) and w == 2 * NP - 1):
                    pool.wait_ge(projected, 16 * w + 16)
                    split_w(w + 1)
                for n in lns:
                    add_bias(n)

            run_slots(pool, slot, add_bias)

        @block.scalar
        def _(act):
            act.dma_start(cond[:, :, :], cond_d).then_inc(ada_in, 16)
            act.dma_start(ada_w[:, :, :, :], ada_d).then_inc(ada_in, 16)
            act.dma_start(cols[:, :], cols_d).then_inc(cols_in, 16)
            act.dma_start(ctx_ln[:, :, :], ctxln_d).then_inc(cols_in, 16)
            act.dma_start(rope[:, :, :, :, :], rope_d).then_inc(rope_in, 16)
            act.dma_start(bias_rows[:, :, :], rows_d.partition_broadcast(128)).then_inc(rows_in, 16)

            def norm(n):
                kind, b, ada = order[n]
                rows = source(n)[1]
                for r in range(KT):
                    act.wait_ge(ln_turned, 2 * n + r + 1)
                    if 2 * n + r > 0:
                        act.wait_ge(ln_split, 2 * n + r)
                    if kind == X:
                        scale, shift = ada_scale[:, ada, r, b:b + 1], ada_shift[:, ada, r, b:b + 1]
                    else:
                        scale, shift = ctx_ln[:, 0, r:r + 1], ctx_ln[:, 1, r:r + 1]
                    act.activation(y[0:rows, :], side_ps[0:rows, :], ACT.Identity, bias=shift, scale=scale)\
                       .then_inc(ln_scaled, 1)

            def keep_v(u, par, tt):
                act.wait_ge(projected, 4 * u + tt + 1)
                act.copy(v[:, par, tt, :], proj_ps[:, 2 * 128:QKV]).then_inc(v_ready, 1)

            def high(u, par, r):
                act.wait_ge(qk_turned, 4 * u + r + 1)
                dst = (q_hi if r < 2 else k_parts)[:, par, r % 2, :]
                act.copy(dst, side_ps).then_inc(qk_high, 1)

            def exp(u, par, i):
                act.wait_ge(maxed, 8 * u + i + 1)
                act.activation(probs[:, i, :], score_ps[i % 2], ACT.Exp, bias=neg_max[:, par, i:i + 1],
                               accum_out=row_sum[:, par, i:i + 1]).then_inc(exped, 1)

            def keep_turned(u, j):
                act.wait_ge(turned, 8 * u + j + 1)
                act.copy(probs_t[:, j, :], turn_ps[j % 2]).then_inc(probs_t_ready, 1)

            act.wait_ge(cols_in, 32)
            act.wait_ge(ada_step, ADA_STEPS)
            norm(0)
            for tt in range(TT):
                keep_v(0, 0, tt)
            for r in range(X_ROUNDS):
                high(0, 0, r)
            for n in range(1, NB):
                norm(n)

            def slot(u, b, w, phase, after, lns, done):
                par, nxt = b % 2, (b + 1) % 2
                for i in range(S_TILES):
                    exp(u, par, i)
                    if i % 2 and after is not None:
                        keep_v(u + 1, nxt, i // 2)
                for j in range(T_BLOCKS):
                    keep_turned(u, j)
                    if j >= TT - 1 and j < T_BLOCKS - 1 and after is not None:
                        high(u + 1, nxt, j - TT + 1)
                for n in lns:
                    norm(n)
                act.wait_ge(averaged, 4 * u + 4)
                act.copy(o_hi[:, :], av_ps).then_inc(o_high, 1)

            run_slots(act, slot, norm)

            act.wait_ge(projected, 4 * UNITS)
            act.wait_ge(ffw_loaded, 32)
            act.copy(w1_hi[:, :, :], w1_raw[:, :, :]).then_inc(ffw_high, 1)
            act.copy(w2_hi[:, :, :], w2_raw[:, :, :]).then_inc(ffw_high, 1)

            with act.Fori(0, NB) as b:
                for f in range(FT):
                    act.wait_ge(hid_mm, 8 * b + f + 1)
                    if f >= 4:
                        act.wait_ge(hid_split, 8 * b + f - 3)
                    act.activation(hid[:, f % 4, :], ps[:, f % 4, :], ACT.Gelu,
                                   bias=cols[:, 8 * KT + f:8 * KT + f + 1]).then_inc(hid_ready, 1)

        @block.tensor
        def _(pe):
            pe.wait_ge(ada_in, 32)
            for m in range(4):
                for kt in range(KT):
                    for kc in range(KT):
                        mm = pe.matmul(out_ps[:, (m * KT + kt) * NB:(m * KT + kt + 1) * NB],
                                       ada_w[:, m, kc, kt * 128:(kt + 1) * 128], cond[:, kc, :],
                                       start=(kc == 0), stop=(kc == KT - 1))
            mm.then_inc(ada_mm, 1)
            pe.wait_ge(ident_ready, 2)

            def parts(out, a_hi, a_lo, b_hi, b_lo, first=True, last=True):
                pe.matmul(out, a_hi, b_hi, start=first, stop=False)
                pe.matmul(out, a_hi, b_lo, start=False, stop=False)
                return pe.matmul(out, a_lo, b_hi, start=False, stop=last)

            def norm(n):
                rows = source(n)[1]
                pe.wait_ge(ln_step, X_READ * (n + 1))
                for r in range(KT):
                    if 2 * n + r > 0:
                        pe.wait_ge(ln_scaled, 2 * n + r)
                    for tt in range(TT):
                        mm = pe.transpose(side_ps[0:rows, tt * 128:(tt + 1) * 128],
                                          z[:, tt, r * rows:(r + 1) * rows], ident[:, :])
                    mm.then_inc(ln_turned, 1)

            def project(u, b, w, phase, tt, first=False):
                cut = slice(tt * 128, (tt + 1) * 128)
                if tt == 0:
                    pe.wait_ge(ln_split, 2 * place[(X, b, phase)] + 2)
                    pe.wait_ge(w_split, w + 1)
                if not (first and tt == 0):
                    pe.wait_ge(roped, 4 * u + tt)
                if phase == 0:
                    for kt in range(KT):
                        c = slice(kt * QKV, (kt + 1) * QKV)
                        mm = parts(proj_ps[:, 0:QKV], xn_hi[:, b, kt, cut], xn_lo[:, b, kt, cut],
                                   w_hi[:, c], w_lo[:, c], kt == 0, kt == KT - 1)
                else:
                    if tt == 0:
                        pe.wait_ge(ln_split, 2 * place[(C, b, 0)] + 2)
                    for kt in range(KT):
                        c = slice(kt * 128, (kt + 1) * 128)
                        parts(proj_ps[:, 0:128], xn_hi[:, b, kt, cut], xn_lo[:, b, kt, cut],
                              w_hi[:, c], w_lo[:, c], kt == 0, kt == KT - 1)
                    for kt in range(KT):
                        c = slice(KT * 128 + kt * 256, KT * 128 + (kt + 1) * 256)
                        mm = parts(proj_ps[:, 128:QKV], ctx_hi[0:CK, b, kt, cut], ctx_lo[0:CK, b, kt, cut],
                                   w_hi[0:CK, c], w_lo[0:CK, c], kt == 0, kt == KT - 1)
                mm.then_inc(projected, 1)

            def turn_qk(u, r, done, first=False):
                if r == 0:
                    pe.wait_ge(rot_ready, 4 * u + 4)
                    pe.wait_ge(ln_scaled, 2 * done)
                if not (first and r == 0):
                    pe.wait_ge(qk_low, 4 * u + r)
                for tt in range(TT):
                    mm = pe.transpose(side_ps[:, tt * 128:(tt + 1) * 128],
                                      rotated[:, tt, r, :, :].rearrange("p a d -> p (a d)"), ident[:, :])
                mm.then_inc(qk_turned, 1)

            def score(u, par, i):
                h, cut = i // TT, slice(i % TT * 128, (i % TT + 1) * 128)
                if i == 0:
                    pe.wait_ge(qk_low, 4 * u + 4)
                if i >= 2:
                    pe.wait_ge(exped, 8 * u + i - 1)
                pe.matmul(score_ps[i % 2], q_hi[:, par, h, cut], k_parts[:, par, h, :], start=True, stop=False)
                pe.matmul(score_ps[i % 2], q_lo[:, par, h, cut], k_parts[:, par, h, :], start=False, stop=True)\
                  .then_inc(scored, 1)

            def turn_probs(u, j):
                h, kt = divmod(j, TT)
                if kt == 0:
                    pe.wait_ge(normed, 8 * u + TT * h + TT)
                if j >= 2:
                    pe.wait_ge(probs_t_ready, 8 * u + j - 1)
                for qt in range(TT):
                    mm = pe.transpose(turn_ps[j % 2][:, qt * 128:(qt + 1) * 128],
                                      probs[:, TT * h + qt, kt * 128:(kt + 1) * 128], ident[:, :])
                mm.then_inc(turned, 1)

            def average(u, par, kt):
                if kt == 0:
                    pe.wait_ge(v_ready, 4 * u + 4)
                pe.wait_ge(probs_t_ready, 8 * u + TT + kt + 1)
                for h in range(2):
                    mm = pe.matmul(av_ps[DH * h:DH * h + DH, :], v[:, par, kt, DH * h:DH * h + DH],
                                   probs_t[:, TT * h + kt, :], start=(kt == 0), stop=(kt == TT - 1))
                mm.then_inc(averaged, 1)

            def project_out(u, w, r):
                if r == 0:
                    pe.wait_ge(o_low, u + 1)
                    pe.wait_ge(wo_split, w + 1)
                else:
                    pe.wait_ge(o_added, 2 * u + 1)
                for t in range(2):
                    cut = slice((2 * r + t) * 128, (2 * r + t + 1) * 128)
                    mm = parts(out_ps[:, t * D:(t + 1) * D], o_hi[:, cut], o_lo[:, cut], wo_hi[:, :], wo_lo[:, :])
                mm.then_inc(o_projected, 1)

            norm(0)
            for tt in range(TT):
                project(0, 0, 0, 0, tt, first=True)
            for r in range(X_ROUNDS):
                turn_qk(0, r, 1, first=True)
            pe.wait_ge(qk_low, X_ROUNDS)
            for n in range(1, NB):
                norm(n)

            def slot(u, b, w, phase, after, lns, done):
                par, b1 = b % 2, (b + 1) % NB
                w1 = w if b < NB - 1 else w + 1
                for i in range(S_TILES):
                    score(u, par, i)
                    if i % 2 and after is not None:
                        project(u + 1, b1, w1, after, i // 2)
                for j in range(T_BLOCKS):
                    turn_probs(u, j)
                    if j >= TT:
                        average(u, par, j - TT)
                    if j >= TT - 1 and j < T_BLOCKS - 1 and after is not None:
                        turn_qk(u + 1, j - TT + 1, done)
                if lns:
                    pe.wait_ge(qk_low, 4 * u + (8 if after is not None else 4))
                for n in lns:
                    norm(n)
                for r in range(2):
                    project_out(u, w, r)

            run_slots(pe, slot, norm)

            pe.wait_ge(ffw_split, 2)
            pe.wait_ge(ln_split, 2 * len(order))
            with pe.Fori(0, NB) as b:
                def hidden(f):
                    if f >= 4:
                        pe.wait_ge(hid_ready, 8 * b + f - 3)
                    cut = slice(f * 128, (f + 1) * 128)
                    for kt in range(KT):
                        hi = xn_hi[:, bass.ds(b, 1), kt, :].rearrange("p a n -> p (a n)")
                        lo = xn_lo[:, bass.ds(b, 1), kt, :].rearrange("p a n -> p (a n)")
                        mm = parts(ps[:, f % 4, :], w1_hi[:, kt, cut], w1_lo[:, kt, cut], hi, lo,
                                   kt == 0, kt == KT - 1)
                    mm.then_inc(hid_mm, 1)

                def down(f):
                    pe.wait_ge(hid_split, 8 * b + f + 1)
                    for tt in range(TT):
                        out = ps[:, 4 + tt // 2, tt % 2 * D:(tt % 2 + 1) * D]
                        cut = slice(tt * 128, (tt + 1) * 128)
                        hi, lo = hid_hi[:, f % 4, cut], hid_lo[:, f % 4, cut]
                        for n, (a, c) in enumerate(((hi, w2_hi), (hi, w2_lo), (lo, w2_hi))):
                            mm = pe.matmul(out, a, c[:, f, :], start=(f == 0 and n == 0 and tt % 2 == 0),
                                           stop=(f == FT - 1 and n == 2), skip_group_check=True)
                    mm.then_inc(y_step, 1)

                hidden(0)
                hidden(1)
                for f in range(FT):
                    if f + 2 < FT:
                        hidden(f + 2)
                    down(f)

        @block.vector
        def _(dve):
            dve.wait_ge(ada_mm, 1)
            dve.wait_ge(cols_in, 32)

            def gamma(a, kt, beta=0):
                at = ((2 * a + beta) * KT + kt) * NB
                return out_ps[:, at:at + NB]

            def col(j, kt):
                return cols[:, j * KT + kt:j * KT + kt + 1]

            sets = [(a, kt) for a in range(2) for kt in range(KT)]
            for a, kt in sets:
                dve.tensor_scalar(ada_g1[:, a, kt, :], gamma(a, kt), col(4 * a + 2, kt), 1.0, ALU.add, ALU.add)\
                   .then_inc(ada_step, 1)
            dve.wait_ge(ada_step, len(sets))
            for a, kt in sets:
                dve.scalar_tensor_tensor(ada_gb[:, a, kt, :], ada_g1[:, a, kt, :], col(4 * a + 1, kt),
                                         gamma(a, kt, 1), ALU.mult, ALU.add).then_inc(ada_step, 1)
            for a, kt in sets:
                dve.tensor_scalar(ada_scale[:, a, kt, :], ada_g1[:, a, kt, :], col(4 * a, kt), None, ALU.mult)\
                   .then_inc(ada_step, 1)
            dve.wait_ge(ada_step, 2 * len(sets))
            for a, kt in sets:
                dve.tensor_scalar(ada_shift[:, a, kt, :], ada_gb[:, a, kt, :], col(4 * a + 3, kt), None, ALU.add)\
                   .then_inc(ada_step, 1)

            def norm(n):
                kind, b, _ = order[n]
                src, rows = source(n)
                sublayer = sum(1 for other in order[:n] if other[0] == X) // NB
                if kind == X and sublayer > 0:
                    dve.wait_ge(o_added, 2 * (4 * (NP * sublayer - 1) + b) + 2)
                for tt in range(TT):
                    dve.bn_stats(stats[:, tt, :], src[:, tt, :]).then_inc(ln_step, 1)
                dve.wait_ge(ln_step, X_READ * n + TT)
                for tt in range(TT):
                    dve.bn_aggr(mean_var[:, tt, :], stats[:, tt, :]).then_inc(ln_step, 1)
                dve.wait_ge(ln_step, X_READ * n + 2 * TT)
                dve.tensor_scalar(var_eps[:, :], mean_var[:, :, 1], EPS, None, ALU.add).then_inc(ln_step, 1)
                at = X_READ * n + 2 * TT + 1
                dve.wait_ge(ln_step, at)
                dve.tensor_scalar(rstd[:, :].bitcast(I32), var_eps[:, :].bitcast(I32), -0.5, RSQRT_GUESS,
                                  ALU.mult, ALU.add).then_inc(ln_step, 1)
                for _ in range(NEWTON):
                    dve.wait_ge(ln_step, at + 1)
                    dve.tensor_tensor(newton[:, :], rstd[:, :], rstd[:, :], ALU.mult).then_inc(ln_step, 1)
                    dve.wait_ge(ln_step, at + 2)
                    dve.scalar_tensor_tensor(newton[:, :], newton[:, :], -0.5, var_eps[:, :], ALU.mult, ALU.mult)\
                       .then_inc(ln_step, 1)
                    dve.wait_ge(ln_step, at + 3)
                    dve.scalar_tensor_tensor(rstd[:, :], newton[:, :], 1.5, rstd[:, :], ALU.add, ALU.mult)\
                       .then_inc(ln_step, 1)
                    at += 3
                dve.wait_ge(ln_step, at + 1)
                for tt in range(TT):
                    dve.tensor_scalar(z[:, tt, 0:KT * rows], src[:, tt, :], mean_var[:, tt, 0:1],
                                      rstd[:, tt:tt + 1], ALU.subtract, ALU.mult).then_inc(ln_step, 1)
                hi, lo = (xn_hi, xn_lo) if kind == X else (ctx_hi, ctx_lo)
                for r in range(KT):
                    dve.wait_ge(ln_scaled, 2 * n + r + 1)
                    dve.tensor_copy(hi[0:rows, b, r, :], y[0:rows, :]).then_inc(ln_rounded, 1)
                    dve.wait_ge(ln_rounded, 2 * n + r + 1)
                    dve.tensor_tensor(lo[0:rows, b, r, :], y[0:rows, :], hi[0:rows, b, r, :], ALU.subtract)\
                       .then_inc(ln_split, 1)

            def rotate(u, tt):
                dve.wait_ge(v_ready, 4 * u + tt + 1)
                if tt >= 2:
                    dve.wait_ge(rot_ready, 4 * u + tt - 1)
                qk = proj_ps[:, 0:2 * 128].rearrange("p (g d) -> p g d", g=4)
                dve.tensor_tensor(rot_a[:, tt % 2, :, :], qk, rope[:, 0, tt, :, :], ALU.mult)
                swapped = proj_ps[:, 0:2 * 128].rearrange("p (g s d) -> p g s d", g=4, s=2)[:, :, ::-1, :]
                dve.tensor_tensor(rot_b[:, tt % 2, :, :].rearrange("p g (s d) -> p g s d", s=2), swapped,
                                  rope[:, 1, tt, :, :].rearrange("p g (s d) -> p g s d", s=2), ALU.mult)\
                   .then_inc(roped, 1)

            def low(u, par, r):
                dve.wait_ge(qk_high, 4 * u + r + 1)
                if r < 2:
                    dve.tensor_tensor(q_lo[:, par, r, :], side_ps, q_hi[:, par, r, :], ALU.subtract)\
                       .then_inc(qk_low, 1)
                else:
                    k = k_parts[DH:128, par, r - 2, :]
                    dve.tensor_tensor(k, side_ps[DH:128, :], k, ALU.subtract).then_inc(qk_low, 1)

            def peak(u, par, i):
                dve.wait_ge(scored, 8 * u + i + 1)
                dve.tensor_reduce(neg_max[:, par, i:i + 1], score_ps[i % 2], AX.X, ALU.max, negate=True)\
                   .then_inc(maxed, 1)

            def invert(u, par, h):
                dve.wait_ge(exped, 8 * u + TT * h + TT)
                cut = slice(TT * h, TT * h + TT)
                dve.reciprocal(row_inv[:, par, cut], row_sum[:, par, cut]).then_inc(inverted, 1)

            def normalise(u, par, i):
                if i % TT == 0:
                    dve.wait_ge(inverted, 2 * u + i // TT + 1)
                dve.tensor_scalar(probs[:, i, :], probs[:, i, :], row_inv[:, par, i:i + 1], None, ALU.mult)\
                   .then_inc(normed, 1)

            dve.wait_ge(x_in[0], 16)
            norm(0)
            dve.wait_ge(rope_in, 16)
            for tt in range(TT):
                rotate(0, tt)
            for r in range(X_ROUNDS):
                low(0, 0, r)
            for n in range(1, NB):
                dve.wait_ge(x_in[n], 16)
                norm(n)
            dve.wait_ge(ctx_loaded, 16 * NB)

            def slot(u, b, w, phase, after, lns, done):
                par, nxt = b % 2, (b + 1) % 2
                prep = after is not None
                for i in range(S_TILES):
                    peak(u, par, i)
                    if i == 4:
                        invert(u, par, 0)
                    if i >= 5 and i != 6:
                        normalise(u, par, i - 5 if i == 5 else 2)
                    if i == 5:
                        normalise(u, par, 1)
                    if i == 7:
                        normalise(u, par, 3)
                    if i % 2 and prep:
                        rotate(u + 1, i // 2)
                invert(u, par, 1)
                for i in range(TT, S_TILES):
                    normalise(u, par, i)
                if prep:
                    for r in range(X_ROUNDS):
                        low(u + 1, nxt, r)
                for n in lns:
                    norm(n)
                dve.wait_ge(o_high, u + 1)
                dve.tensor_tensor(o_lo[:, :], av_ps, o_hi[:, :], ALU.subtract).then_inc(o_low, 1)
                dve.wait_ge(biased, NB * phase + b + 1)
                for r in range(2):
                    dve.wait_ge(o_projected, 2 * u + r + 1)
                    rows = x[:, b, 2 * r:2 * r + 2, :]
                    dve.tensor_tensor(rows, out_ps.rearrange("p (t d) -> p t d", d=D), rows, ALU.add)\
                       .then_inc(o_added, 1)

            run_slots(dve, slot, norm)

            dve.wait_ge(ffw_high, 1)
            dve.tensor_tensor(w1_lo[:, :, :], w1_raw[:, :, :], w1_hi[:, :, :], ALU.subtract).then_inc(ffw_split, 1)
            dve.wait_ge(ffw_high, 2)
            dve.tensor_tensor(w2_lo[:, :, :], w2_raw[:, :, :], w2_hi[:, :, :], ALU.subtract).then_inc(ffw_split, 1)
            dve.wait_ge(biased, 3 * NB)
            with dve.Fori(0, NB) as b:
                for f in range(FT):
                    dve.wait_ge(hid_ready, 8 * b + f + 1)
                    if f >= 4:
                        dve.wait_ge(y_step, 8 * b + f - 3)
                    dve.tensor_copy(hid_hi[:, f % 4, :], hid[:, f % 4, :]).then_inc(hid_rounded, 1)
                    dve.wait_ge(hid_rounded, 8 * b + f + 1)
                    dve.tensor_tensor(hid_lo[:, f % 4, :], hid[:, f % 4, :], hid_hi[:, f % 4, :], ALU.subtract)\
                       .then_inc(hid_split, 1)
                dve.wait_ge(y_step, 8 * b + 8)
                rows = x[:, bass.ds(b, 1), :, :].rearrange("p a t d -> p (a t d)")
                dve.tensor_tensor(rows, ps[:, 4:6, :].rearrange("p a n -> p (a n)"), rows, ALU.add)\
                   .then_inc(y_added, 1)


def rotation_table():
    import numpy as np
    inv = np.float32(1.0) / np.float32(10000.0) ** (np.arange(0, DH, 2, dtype=np.float32) / np.float32(DH))
    angle = np.arange(N, dtype=np.float32)[:, None] * inv[None, :]
    cos, sin = np.cos(angle), np.sin(angle)
    both = np.stack([np.concatenate([cos, cos], 1), np.concatenate([-sin, sin], 1)])
    both = both.reshape(2, TT, 128, 1, DH).transpose(2, 0, 1, 3, 4)
    factor = np.array([DH ** -0.5] * 2 + [1.0] * 2, np.float32).reshape(1, 1, 1, 4, 1)
    return np.ascontiguousarray(both * factor, np.float32)


def kernel(**inputs):
    import numpy as np
    import concourse.bacc as bacc
    from concourse.bass_utils import run_bass_kernel_spmd

    def get(name):
        return np.asarray(inputs[name if name in inputs else "L0_xcond_" + name])

    def by_rows(a, tiles):
        return a.reshape(tiles, -1, a.shape[-1]).transpose(1, 0, 2)

    def pairs(a, apart):
        a = a.reshape(-1, NP, 2, DH // 2, 2) if apart else a.reshape(-1, NP, 2, 2, DH // 2)
        if apart:
            a = a.transpose(0, 1, 2, 4, 3)
        return a.reshape(-1, NP, 128).transpose(1, 0, 2)

    mid = H * DH
    pack = np.zeros((2 * NP, 128, WPACK), np.float32)
    for first, kind in ((0, "sa"), (CROSS, "ca")):
        wq, wkv, wo = get(kind + "_wq"), get(kind + "_wkv"), get(kind + "_wo")
        q, k, v = pairs(wq, True), pairs(wkv[:, :mid], True), pairs(wkv[:, mid:], False)
        for p in range(NP):
            if first == 0:
                qkv = by_rows(np.concatenate([q[p], k[p], v[p]], 1), KT)
                pack[p, :, 0:WQKV] = qkv.reshape(128, WQKV)
            else:
                pack[first + p, :, 0:KT * 128] = by_rows(q[p], KT).reshape(128, KT * 128)
                kv = by_rows(np.concatenate([k[p], v[p]], 1), KT)
                pack[first + p, 0:CK, KT * 128:WQKV] = kv.reshape(CK, KT * 256)
            pack[first + p, :, WQKV:WPACK] = wo[p * 128:(p + 1) * 128]
    columns = [get(n).reshape(KT, 128).T for n in
               ("ln1_w", "ln1_b", "g1_b", "b1_b", "ln2_w", "ln2_b", "g2_b", "b2_b")]
    columns.append(get("ff_b1").reshape(FT, 128).T)
    arrays = {
        "x_dram": get("x"),
        "ctx_dram": get("ctx_768"),
        "pack_dram": pack,
        "cond_dram": by_rows(get("cond_1024").T, KT),
        "ada_dram": np.stack([by_rows(get(n), KT) for n in ("g1_w", "b1_w", "g2_w", "b2_w")], 1),
        "cols_dram": np.concatenate(columns, 1),
        "ctxln_dram": np.stack([get(n).reshape(KT, CK).T for n in ("ca_lnc_w", "ca_lnc_b")], 1),
        "rows_dram": np.stack([get(n) for n in ("sa_bo", "ca_bo", "ff_b2")]),
        "w1_dram": by_rows(get("ff_w1"), KT),
        "w2_dram": by_rows(get("ff_w2"), FT),
        "rope_dram": rotation_table(),
    }
    arrays = {n: np.ascontiguousarray(a) for n, a in arrays.items()}
    nc = bacc.Bacc("TRN2", target_bir_lowering=False, num_devices=1)
    args = [nc.dram_tensor(n, a.shape, mybir.dt.from_np(a.dtype), kind="ExternalInput").ap()
            for n, a in arrays.items()]
    out = nc.dram_tensor("out", (NB, N, D), F32, kind="ExternalOutput").ap()
    build(nc, *args, out)
    return run_bass_kernel_spmd(nc, [arrays], core_ids=[0]).results[0]["out"]
```

```python
import concourse.bass as bass
from concourse import mybir
from contextlib import ExitStack

F32 = mybir.dt.float32
F32R = mybir.dt.float32r
I32 = mybir.dt.int32
ALU = mybir.AluOpType
ACT = mybir.ActivationFunctionType
AX = mybir.AxisListType

NB = 4
N = 512
TT = N // 128
D = 256
KT = D // 128
DC = 192
CK = DC // KT
DH = 64
H = 16
NP = H // 2
FF = 4 * D
FT = FF // 128
EPS = 1e-5
NEWTON = 3
RSQRT_GUESS = float(0x5F3759DF)
QKV = 3 * 128
WQKV = KT * QKV
WPACK = WQKV + D
T_BLOCKS = 2 * TT
S_TILES = 2 * TT
X_ROUNDS = 4
UNITS = NB * 2 * NP
RING = (("S", 0, 1), ("S", 1, 1), ("S", 2, 1), ("T", 4, 0), ("S", 3, 1), ("T", 5, 0),
        ("T", 6, 0), ("T", 7, 0), ("S", 4, 1), ("S", 5, 1), ("S", 6, 1), ("S", 7, 1),
        ("T", 0, 1), ("T", 1, 1), ("T", 2, 1), ("T", 3, 1))
SIDE = (("X", 2, 1), ("X", 3, 1), ("X", 0, 2), ("X", 1, 2), ("O", 1, 0))


def build(nc, x_d, ctx_d, pack_d, cond_d, ada_d, cols_d, ctxln_d, rows_d, w1_d, w2_d, rope_d, out_d):
    stack = ExitStack()
    with stack:
        attention_only = ExitStack()

        def sb(name, shape, dt=F32, where=stack):
            return where.enter_context(nc.sbuf_tensor(name, shape, dt))

        def sem(name):
            return stack.enter_context(nc.semaphore(name))

        x = sb("x", [128, NB, TT, D])
        xn_hi = sb("xn_hi", [128, NB, KT, N], F32R)
        xn_lo = sb("xn_lo", [128, NB, KT, N], F32R)
        ident = sb("ident", [128, 128])
        zero = sb("zero", [128, 1])
        cols = sb("cols", [128, 8 * KT + FT])
        cond = sb("cond", [128, KT, NB])
        ada_scale = sb("ada_scale", [128, 2, KT, NB])
        ada_shift = sb("ada_shift", [128, 2, KT, NB])
        ada_g1 = sb("ada_g1", [128, 2, KT, NB])
        ada_gb = sb("ada_gb", [128, 2, KT, NB])
        bias_rows = sb("bias_rows", [128, 3, D])
        stats = sb("stats", [128, TT, 6])
        mean_var = sb("mean_var", [128, TT, 2])
        rstd = sb("rstd", [128, TT])
        var_eps = sb("var_eps", [128, TT])
        newton = sb("newton", [128, TT])
        z = sb("z", [128, TT, D])
        y = sb("y", [128, N])

        def asb(name, shape, dt=F32):
            return sb(name, shape, dt, attention_only)

        ctx_hi = asb("ctx_hi", [128, NB, KT, N], F32R)
        ctx_lo = asb("ctx_lo", [128, NB, KT, N], F32R)
        ctx_in = asb("ctx_rows", [128, NB - 1, TT, DC])
        ctx_ln = asb("ctx_ln", [CK, 2, KT])
        ada_w = asb("ada_w", [128, 4, KT, D])
        rope = asb("rope", [128, 2, TT, 4, DH])
        w_raw = asb("w_raw", [128, WPACK])
        w_hi = asb("w_hi", [128, WQKV], F32R)
        w_lo = asb("w_lo", [128, WQKV], F32R)
        wo_hi = asb("wo_hi", [128, D], F32R)
        wo_lo = asb("wo_lo", [128, D], F32R)
        rot_a = asb("rot_a", [128, 2, 4, DH])
        rot_b = asb("rot_b", [128, 2, 4, DH])
        rotated = asb("rotated", [128, TT, 4, 2, DH])
        q_hi = asb("q_hi", [128, 2, 2, N], F32R)
        q_lo = asb("q_lo", [128, 2, 2, N], F32R)
        k_parts = asb("k_parts", [128, 2, 2, N], F32R)
        v = asb("v", [128, NB, TT, 128])
        probs = asb("probs", [128, S_TILES, N])
        probs_t = asb("probs_t", [128, T_BLOCKS, N])
        neg_max = asb("neg_max", [128, 2, S_TILES])
        row_sum = asb("row_sum", [128, 2, S_TILES])
        row_inv = asb("row_inv", [128, 2, S_TILES])
        o_hi = asb("o_hi", [128, N], F32R)
        o_lo = asb("o_lo", [128, N], F32R)
        attention_only.close()

        w1_hi = sb("w1_hi", [128, KT, FF], F32R)
        w1_lo = sb("w1_lo", [128, KT, FF], F32R)
        w2_hi = sb("w2_hi", [128, FT, D], F32R)
        w2_lo = sb("w2_lo", [128, FT, D], F32R)
        w1_raw = sb("w1_raw", [128, KT, FF])
        w2_raw = sb("w2_raw", [128, FT, D])
        hid = sb("hid", [128, 4, N])
        hid_hi = sb("hid_hi", [128, 4, N], F32R)
        hid_lo = sb("hid_lo", [128, 4, N], F32R)

        ps = stack.enter_context(nc.psum_tensor("ps", [128, 8, N], F32))
        RING_AT = {(kind, n): pos for pos, (kind, n, _) in enumerate(RING)}

        def ring_ps(kind, n):
            return ps[:, RING_AT[(kind, n)] % 4, :]

        av_ps = ps[:, 4, :]
        proj_ps = (ps[:, 5, :], ps[:, 7, :])
        side_ps = ps[:, 6, :]
        out_ps = (av_ps, side_ps)

        ada_in = sem("ada_in")
        cols_in = sem("cols_in")
        rope_in = sem("rope_in")
        rows_in = sem("rows_in")
        x_in = [sem(f"x_in{b}") for b in range(NB)]
        ctx_loaded = sem("ctx_loaded")
        ident_ready = sem("ident_ready")
        zero_ready = sem("zero_ready")
        ada_mm = sem("ada_mm")
        ada_step = sem("ada_step")
        ln_step = sem("ln_step")
        ln_turned = sem("ln_turned")
        ln_scaled = sem("ln_scaled")
        ln_rounded = sem("ln_rounded")
        ln_split = sem("ln_split")
        biased = sem("biased")
        w_loaded = sem("w_loaded")
        w_step = sem("w_step")
        w_split = sem("w_split")
        wo_step = sem("wo_step")
        wo_split = sem("wo_split")
        projected = sem("projected")
        roped = sem("roped")
        v_ready = sem("v_ready")
        rot_ready = sem("rot_ready")
        qk_turned = sem("qk_turned")
        qk_high = sem("qk_high")
        qk_low = sem("qk_low")
        scored = sem("scored")
        maxed = sem("maxed")
        exped = sem("exped")
        inverted = sem("inverted")
        normed = sem("normed")
        turned = sem("turned")
        probs_t_ready = sem("probs_t_ready")
        averaged = sem("averaged")
        o_high = sem("o_high")
        o_low = sem("o_low")
        o_projected = sem("o_projected")
        o_added = sem("o_added")
        ffw_loaded = sem("ffw_loaded")
        ffw_high = sem("ffw_high")
        ffw_split = sem("ffw_split")
        hid_mm = sem("hid_mm")
        hid_ready = sem("hid_ready")
        hid_rounded = sem("hid_rounded")
        hid_split = sem("hid_split")
        y_step = sem("y_step")
        y_added = sem("y_added")
        stored = sem("stored")

        X, C = 0, 1
        order = [(X, b, 0) for b in range(NB)]
        order += [(kind, b, 0) for b in range(NB) for kind in (C, X)]
        order += [(X, b, 1) for b in range(NB)]

        def norm_of(kind, sublayer, b):
            if kind == C:
                return NB + 2 * b
            return (b, NB + 2 * b + 1, 3 * NB + b)[sublayer]

        X_READ = 3 * TT + 2 + 3 * NEWTON

        def unit(w, b, phase, ahead):
            b += ahead
            if b >= NB:
                w, b = w + 1, b - NB
            if isinstance(w, int):
                if not 0 <= w < 2 * NP:
                    return None
                phase = w // NP
            return 4 * w + b, b, w, phase

        def run_slots(eng, slot):
            def step(w, phase, batches=range(NB)):
                for b in batches:
                    slot(w, b, unit(w, b, phase, 0), unit(w, b, phase, 1), unit(w, b, phase, 2))

            step(-1, 0, range(NB - 2, NB))
            for phase in range(2):
                first = phase * NP
                step(first, phase)
                with eng.Fori(first + 1, first + NP - 1) as w:
                    step(w, phase)
                step(first + NP - 1, phase)

        def there(step):
            return lambda x, *which: step(x, *which) if x is not None else None

        def wait_for(eng, signal, count):
            if not (isinstance(count, int) and count <= 0):
                eng.wait_ge(signal, count)

        def prior(uses, pos, u):
            stride = 4 if uses is RING else 1
            for back in range(stride, 3 * len(uses), stride):
                slots_back, at = divmod(pos - back, len(uses))
                kind, n, ahead = uses[at]
                v = u + (slots_back + ahead)
                if not isinstance(v, int) or 0 <= v < UNITS:
                    return kind, n, v
            return None

        def mid_norm(w, b):
            if not isinstance(w, int):
                return []
            if w in (NP - 1, 2 * NP - 1) and b > 0:
                return [norm_of(X, w // NP + 1, b - 1)]
            return [norm_of(X, 1, NB - 1)] if (w, b) == (NP, 0) else []

        def end_norm(w, b):
            if isinstance(w, int) and 4 * w + b in (-2, -1, 0):
                return [4 * w + b + 3]
            return [norm_of(C, 0, b)] if isinstance(w, int) and w == NP - 1 else []

        def whole_norm(w, b):
            return [norm_of(X, w // NP + 1, b)] if isinstance(w, int) and w in (NP - 1, 2 * NP - 1) else []

        def source(n):
            kind, b, _ = order[n]
            return (x[:, b, :, :], 128) if kind == X else (ctx_in[:, b % (NB - 1), :, :], CK)

        ADA_STEPS = 4 * 2 * KT
        block = stack.enter_context(nc.Block())

        @block.sync
        def _(sp):
            sp.dma_start(x[:, 0, :, :], x_d[0].rearrange("(t p) d -> p t d", p=128)).then_inc(x_in[0], 16)
            sp.dma_start(w_raw[:, :], pack_d[0]).then_inc(w_loaded, 16)
            for b in range(1, NB):
                sp.dma_start(x[:, b, :, :], x_d[b].rearrange("(t p) d -> p t d", p=128)).then_inc(x_in[b], 16)
            for b in range(NB - 1):
                sp.dma_start(ctx_in[:, b, :, :], ctx_d[b].rearrange("(t p) d -> p t d", p=128))\
                  .then_inc(ctx_loaded, 16)
            for first, end in ((1, NP + 1), (NP + 1, 2 * NP)):
                with sp.Fori(first, end) as w:
                    sp.wait_ge(w_split, w)
                    sp.wait_ge(wo_split, w)
                    sp.dma_start(w_raw[:, :], pack_d[bass.ds(w, 1), :, :].rearrange("a p c -> p (a c)"))\
                      .then_inc(w_loaded, 16)
                if first == 1:
                    sp.wait_ge(ln_split, 2 * norm_of(C, 0, 0) + 2)
                    sp.dma_start(ctx_in[:, 0, :, :], ctx_d[NB - 1].rearrange("(t p) d -> p t d", p=128))\
                      .then_inc(ctx_loaded, 16)
            sp.wait_ge(ln_split, 2 * norm_of(C, 0, NB - 1) + 2)
            sp.dma_start(w1_raw[:, :, :], w1_d).then_inc(ffw_loaded, 16)
            sp.dma_start(w2_raw[:, :, :], w2_d).then_inc(ffw_loaded, 16)
            with sp.Fori(0, NB) as b:
                sp.wait_ge(y_added, b + 1)
                sp.dma_start(out_d[bass.ds(b, 1), :, :].rearrange("a (t p) d -> p (a t) d", p=128),
                             x[:, bass.ds(b, 1), :, :].rearrange("p a t d -> p (a t) d")).then_inc(stored, 16)
            sp.wait_ge(stored, 16 * NB)

        @block.gpsimd
        def _(pool):
            pool.memset(ident[:, :], 0.0).then_inc(ident_ready, 1)
            pool.memset(zero[:, :], 0.0).then_inc(zero_ready, 1)
            pool.wait_ge(ident_ready, 1)
            pool.affine_select(out=ident[:, :], in_=ident[:, :], compare_op=ALU.not_equal, fill=1.0,
                               base=0, pattern=[[-1, 128]], channel_multiplier=1).then_inc(ident_ready, 1)

            @there
            def split_wo(x):
                u, b, w, _ = x
                if b > 0:
                    return
                raw = w_raw[:, WQKV:WPACK]
                pool.wait_ge(w_loaded, 16 * w + 16)
                wait_for(pool, o_projected, 2 * u)
                pool.tensor_tensor(wo_hi[:, :], raw, zero[:, :].broadcast_to([128, D]), ALU.add).then_inc(wo_step, 1)
                pool.wait_ge(wo_step, w + 1)
                pool.tensor_tensor(wo_lo[:, :], raw, wo_hi[:, :], ALU.subtract)\
                    .then_inc(wo_split, 1)

            @there
            def add_rotation(x, tt):
                u = x[0]
                pool.wait_ge(roped, 4 * u + tt + 1)
                if tt == 0:
                    wait_for(pool, qk_turned, 4 * u)
                a = rot_a[:, tt % 2, :, :].unsqueeze(2).broadcast_to([128, 4, 2, DH])
                c = rot_b[:, tt % 2, :, :].unsqueeze(2).broadcast_to([128, 4, 2, DH])
                pool.tensor_tensor(rotated[:, tt, :, :, :], a, c, ALU.add).then_inc(rot_ready, 1)

            def add_bias(n):
                b = order[n][1]
                sublayer = sum(1 for kind, _, _ in order[:n] if kind == X) // NB
                pool.wait_ge(ln_step, X_READ * (n + 1))
                pool.tensor_tensor(x[:, b, :, :], x[:, b, :, :],
                                   bias_rows[:, sublayer, :].unsqueeze(1).broadcast_to([128, TT, D]),
                                   ALU.add).then_inc(biased, 1)

            def slot(w, b, now, nxt, later):
                add_rotation(later, 0)
                add_rotation(later, 1)
                split_wo(now)
                add_rotation(later, 2)
                add_rotation(later, 3)
                for n in whole_norm(w, b):
                    add_bias(n)
                for n in end_norm(w, b):
                    if n < NB:
                        add_bias(n)

            pool.wait_ge(zero_ready, 1)
            pool.wait_ge(rows_in, 16)
            add_bias(0)
            run_slots(pool, slot)

        @block.scalar
        def _(act):
            act.dma_start(cond[:, :, :], cond_d).then_inc(ada_in, 16)
            act.dma_start(ada_w[:, :, :, :], ada_d).then_inc(ada_in, 16)
            act.dma_start(cols[:, :], cols_d).then_inc(cols_in, 16)
            act.dma_start(ctx_ln[:, :, :], ctxln_d).then_inc(cols_in, 16)
            act.dma_start(rope[:, :, :, :, :], rope_d).then_inc(rope_in, 16)
            act.dma_start(bias_rows[:, :, :], rows_d.partition_broadcast(128)).then_inc(rows_in, 16)

            def norm(n):
                kind, b, ada = order[n]
                rows = source(n)[1]
                for r in range(KT):
                    act.wait_ge(ln_turned, 2 * n + r + 1)
                    if 2 * n + r > 0:
                        act.wait_ge(ln_split, 2 * n + r)
                    if kind == X:
                        scale, shift = ada_scale[:, ada, r, b:b + 1], ada_shift[:, ada, r, b:b + 1]
                    else:
                        scale, shift = ctx_ln[:, 0, r:r + 1], ctx_ln[:, 1, r:r + 1]
                    act.activation(y[0:rows, :], side_ps[0:rows, :], ACT.Identity, bias=shift, scale=scale)\
                       .then_inc(ln_scaled, 1)

            @there
            def keep_v(x, tt):
                u, b = x[:2]
                act.wait_ge(projected, 4 * u + tt + 1)
                act.copy(v[:, b, tt, :], proj_ps[tt % 2][:, 2 * 128:QKV]).then_inc(v_ready, 1)

            @there
            def high(x, r):
                u, b = x[:2]
                act.wait_ge(qk_turned, 4 * u + r + 1)
                dst = (k_parts if r % 2 else q_hi)[:, b % 2, r // 2, :]
                act.copy(dst, side_ps).then_inc(qk_high, 1)

            @there
            def exp(x, i):
                u, par = x[0], x[1] % 2
                act.wait_ge(maxed, 8 * u + i + 1)
                if i % TT == 0:
                    wait_for(act, turned, 8 * u - 8 + i + TT)
                act.activation(probs[:, i, :], ring_ps("S", i), ACT.Exp, bias=neg_max[:, par, i:i + 1],
                               accum_out=row_sum[:, par, i:i + 1]).then_inc(exped, 1)

            @there
            def keep_turned(x, j):
                u = x[0]
                act.wait_ge(turned, 8 * u + j + 1)
                if j < TT:
                    wait_for(act, averaged, 4 * u - 4 + j + 1)
                act.copy(probs_t[:, j, :], ring_ps("T", j)).then_inc(probs_t_ready, 1)

            @there
            def high_o(x):
                act.wait_ge(averaged, 4 * x[0] + 4)
                act.copy(o_hi[:, :], av_ps).then_inc(o_high, 1)

            def next_weights(w):
                act.wait_ge(w_loaded, 16 * w + 16)
                act.copy(w_hi[:, :], w_raw[:, 0:WQKV]).then_inc(w_step, 1)

            @there
            def round_w(x):
                u, b, w, _ = x
                if b == NB - 1 and not (isinstance(w, int) and w == 2 * NP - 1):
                    act.wait_ge(projected, 4 * u + 4)
                    next_weights(w + 1)

            def slot(w, b, now, nxt, later):
                keep_turned(now, 3)
                keep_v(later, 0)
                high(nxt, 2)
                exp(nxt, 0)
                keep_v(later, 1)
                keep_v(later, 2)
                exp(nxt, 1)
                high(nxt, 3)
                keep_turned(now, 4)
                exp(nxt, 2)
                keep_v(later, 3)
                round_w(later)
                exp(nxt, 3)
                keep_turned(now, 5)
                keep_turned(now, 6)
                keep_turned(now, 7)
                exp(nxt, 4)
                for n in mid_norm(w, b):
                    norm(n)
                high(later, 0)
                exp(nxt, 5)
                exp(nxt, 6)
                high_o(now)
                high(later, 1)
                exp(nxt, 7)
                keep_turned(nxt, 0)
                keep_turned(nxt, 1)
                keep_turned(nxt, 2)
                for n in end_norm(w, b):
                    norm(n)
                if isinstance(w, int) and (w, b) == (2 * NP - 1, NB - 2):
                    act.wait_ge(projected, 4 * UNITS)
                    act.wait_ge(ffw_loaded, 32)
                    act.copy(w1_hi[:, :, :], w1_raw[:, :, :]).then_inc(ffw_high, 1)
                    act.copy(w2_hi[:, :, :], w2_raw[:, :, :]).then_inc(ffw_high, 1)

            next_weights(0)
            act.wait_ge(cols_in, 32)
            act.wait_ge(ada_step, ADA_STEPS)
            norm(0)
            run_slots(act, slot)
            norm(len(order) - 1)

            with act.Fori(0, NB) as b:
                for f in range(FT):
                    act.wait_ge(hid_mm, 8 * b + f + 1)
                    if f >= 4:
                        act.wait_ge(hid_split, 8 * b + f - 3)
                    act.activation(hid[:, f % 4, :], ps[:, f % 4, :], ACT.Gelu,
                                   bias=cols[:, 8 * KT + f:8 * KT + f + 1]).then_inc(hid_ready, 1)

        @block.tensor
        def _(pe):
            pe.wait_ge(ada_in, 32)
            for m in range(4):
                for kt in range(KT):
                    for kc in range(KT):
                        mm = pe.matmul(proj_ps[1][:, (m * KT + kt) * NB:(m * KT + kt + 1) * NB],
                                       ada_w[:, m, kc, kt * 128:(kt + 1) * 128], cond[:, kc, :],
                                       start=(kc == 0), stop=(kc == KT - 1))
            mm.then_inc(ada_mm, 1)
            pe.wait_ge(ident_ready, 2)

            def parts(out, a_hi, a_lo, b_hi, b_lo, first=True, last=True):
                pe.matmul(out, a_hi, b_hi, start=first, stop=False)
                pe.matmul(out, a_hi, b_lo, start=False, stop=False)
                return pe.matmul(out, a_lo, b_hi, start=False, stop=last)

            def norm(n):
                rows = source(n)[1]
                pe.wait_ge(ln_step, X_READ * (n + 1))
                for r in range(KT):
                    if 2 * n + r > 0:
                        pe.wait_ge(ln_scaled, 2 * n + r)
                    for tt in range(TT):
                        mm = pe.transpose(side_ps[0:rows, tt * 128:(tt + 1) * 128],
                                          z[:, tt, r * rows:(r + 1) * rows], ident[:, :])
                    mm.then_inc(ln_turned, 1)

            @there
            def project(x, tt):
                u, b, w, phase = x
                cut = slice(tt * 128, (tt + 1) * 128)
                if tt == 0:
                    pe.wait_ge(ln_split, 2 * norm_of(X, phase, b) + 2)
                    pe.wait_ge(w_split, w + 1)
                wait_for(pe, roped, 4 * u + tt - 1)
                out = proj_ps[tt % 2]
                if phase == 0:
                    for kt in range(KT):
                        c = slice(kt * QKV, (kt + 1) * QKV)
                        mm = parts(out[:, 0:QKV], xn_hi[:, b, kt, cut], xn_lo[:, b, kt, cut],
                                   w_hi[:, c], w_lo[:, c], kt == 0, kt == KT - 1)
                else:
                    if tt == 0:
                        pe.wait_ge(ln_split, 2 * norm_of(C, 0, b) + 2)
                    for kt in range(KT):
                        c = slice(kt * 128, (kt + 1) * 128)
                        parts(out[:, 0:128], xn_hi[:, b, kt, cut], xn_lo[:, b, kt, cut],
                              w_hi[:, c], w_lo[:, c], kt == 0, kt == KT - 1)
                    for kt in range(KT):
                        c = slice(KT * 128 + kt * 256, KT * 128 + (kt + 1) * 256)
                        mm = parts(out[:, 128:QKV], ctx_hi[0:CK, b, kt, cut], ctx_lo[0:CK, b, kt, cut],
                                   w_hi[0:CK, c], w_lo[0:CK, c], kt == 0, kt == KT - 1)
                mm.then_inc(projected, 1)

            def claim_side(pos, u):
                before = prior(SIDE, pos, u)
                if before is not None:
                    kind, n, v = before
                    if kind == "X":
                        wait_for(pe, qk_low, 4 * v + n + 1)
                    else:
                        wait_for(pe, o_added, 2 * v + 2)

            @there
            def turn_qk(x, r):
                u = x[0]
                if r == 0:
                    pe.wait_ge(rot_ready, 4 * u + 4)
                pos = [use[:2] for use in SIDE].index(("X", r))
                claim_side(pos, u - SIDE[pos][2])
                for tt in range(TT):
                    mm = pe.transpose(side_ps[:, tt * 128:(tt + 1) * 128],
                                      rotated[:, tt, 2 * (r % 2) + r // 2, :, :].rearrange("p a d -> p (a d)"),
                                      ident[:, :])
                mm.then_inc(qk_turned, 1)

            def claim(kind, n, u):
                pos = RING_AT[(kind, n)]
                before = prior(RING, pos, u - RING[pos][2])
                if before is not None:
                    was, m, v = before
                    wait_for(pe, exped if was == "S" else probs_t_ready, 8 * v + m + 1)
                return ps[:, pos % 4, :]

            @there
            def score(x, i):
                u, par = x[0], x[1] % 2
                h, cut = i // TT, slice(i % TT * 128, (i % TT + 1) * 128)
                if i % TT == 0:
                    pe.wait_ge(qk_low, 4 * u + 2 * h + 2)
                bank = claim("S", i, u)
                pe.matmul(bank, q_hi[:, par, h, cut], k_parts[:, par, h, :], start=True, stop=False)
                pe.matmul(bank, q_lo[:, par, h, cut], k_parts[:, par, h, :], start=False, stop=True)\
                  .then_inc(scored, 1)

            @there
            def turn_probs(x, j):
                u = x[0]
                h, kt = divmod(j, TT)
                if kt == 0:
                    pe.wait_ge(normed, 8 * u + TT * h + TT)
                bank = claim("T", j, u)
                for qt in range(TT):
                    mm = pe.transpose(bank[:, qt * 128:(qt + 1) * 128],
                                      probs[:, TT * h + qt, kt * 128:(kt + 1) * 128], ident[:, :])
                mm.then_inc(turned, 1)

            @there
            def average(x, kt):
                u, b = x[:2]
                if kt == 0:
                    pe.wait_ge(v_ready, 4 * u + 4)
                    wait_for(pe, o_added, 2 * u - 1)
                pe.wait_ge(probs_t_ready, 8 * u + TT + kt + 1)
                for h in range(2):
                    mm = pe.matmul(av_ps[DH * h:DH * h + DH, :], v[:, b, kt, DH * h:DH * h + DH],
                                   probs_t[:, TT * h + kt, :], start=(kt == 0), stop=(kt == TT - 1))
                mm.then_inc(averaged, 1)

            @there
            def project_out(x, r):
                u, _, w, _ = x
                if r == 0:
                    pe.wait_ge(o_low, u + 1)
                    pe.wait_ge(wo_split, w + 1)
                else:
                    claim_side([use[:2] for use in SIDE].index(("O", r)), u)
                for t in range(2):
                    cut = slice((2 * r + t) * 128, (2 * r + t + 1) * 128)
                    mm = parts(out_ps[r][:, t * D:(t + 1) * D], o_hi[:, cut], o_lo[:, cut], wo_hi[:, :], wo_lo[:, :])
                mm.then_inc(o_projected, 1)

            def norm_in_slot(n, pos, u):
                claim_side(pos, u)
                norm(n)
                pe.wait_ge(ln_scaled, 2 * n + 2)

            def slot(w, b, now, nxt, later):
                score(nxt, 0)
                project(later, 0)
                score(nxt, 1)
                turn_qk(nxt, 2)
                project(later, 1)
                score(nxt, 2)
                project(later, 2)
                turn_qk(nxt, 3)
                turn_probs(now, 4)
                score(nxt, 3)
                project(later, 3)
                turn_probs(now, 5)
                average(now, 0)
                turn_probs(now, 6)
                turn_probs(now, 7)
                score(nxt, 4)
                score(nxt, 5)
                average(now, 1)
                score(nxt, 6)
                for n in mid_norm(w, b):
                    norm_in_slot(n, [use[:2] for use in SIDE].index(("X", 0)), 4 * w + b)
                turn_qk(later, 0)
                average(now, 2)
                average(now, 3)
                score(nxt, 7)
                turn_qk(later, 1)
                turn_probs(nxt, 0)
                turn_probs(nxt, 1)
                turn_probs(nxt, 2)
                project_out(now, 0)
                turn_probs(nxt, 3)
                project_out(now, 1)
                for n in end_norm(w, b):
                    norm_in_slot(n, len(SIDE), 4 * w + b)

            norm(0)
            pe.wait_ge(ln_scaled, 2)
            run_slots(pe, slot)
            norm_in_slot(len(order) - 1, 0, UNITS)

            pe.wait_ge(ffw_split, 2)
            pe.wait_ge(ln_split, 2 * len(order))
            with pe.Fori(0, NB) as b:
                def hidden(f):
                    if f >= 4:
                        pe.wait_ge(hid_ready, 8 * b + f - 3)
                    cut = slice(f * 128, (f + 1) * 128)
                    for kt in range(KT):
                        hi = xn_hi[:, bass.ds(b, 1), kt, :].rearrange("p a n -> p (a n)")
                        lo = xn_lo[:, bass.ds(b, 1), kt, :].rearrange("p a n -> p (a n)")
                        mm = parts(ps[:, f % 4, :], w1_hi[:, kt, cut], w1_lo[:, kt, cut], hi, lo,
                                   kt == 0, kt == KT - 1)
                    mm.then_inc(hid_mm, 1)

                def down(f):
                    pe.wait_ge(hid_split, 8 * b + f + 1)
                    for tt in range(TT):
                        out = ps[:, 4 + tt // 2, tt % 2 * D:(tt % 2 + 1) * D]
                        cut = slice(tt * 128, (tt + 1) * 128)
                        hi, lo = hid_hi[:, f % 4, cut], hid_lo[:, f % 4, cut]
                        for n, (a, c) in enumerate(((hi, w2_hi), (hi, w2_lo), (lo, w2_hi))):
                            mm = pe.matmul(out, a, c[:, f, :], start=(f == 0 and n == 0 and tt % 2 == 0),
                                           stop=(f == FT - 1 and n == 2), skip_group_check=True)
                    mm.then_inc(y_step, 1)

                hidden(0)
                hidden(1)
                for f in range(FT):
                    if f + 2 < FT:
                        hidden(f + 2)
                    down(f)

        @block.vector
        def _(dve):
            dve.wait_ge(ada_mm, 1)
            dve.wait_ge(cols_in, 32)

            def gamma(a, kt, beta=0):
                at = ((2 * a + beta) * KT + kt) * NB
                return proj_ps[1][:, at:at + NB]

            def col(j, kt):
                return cols[:, j * KT + kt:j * KT + kt + 1]

            sets = [(a, kt) for a in range(2) for kt in range(KT)]
            for a, kt in sets:
                dve.tensor_scalar(ada_g1[:, a, kt, :], gamma(a, kt), col(4 * a + 2, kt), 1.0, ALU.add, ALU.add)\
                   .then_inc(ada_step, 1)
            dve.wait_ge(ada_step, len(sets))
            for a, kt in sets:
                dve.scalar_tensor_tensor(ada_gb[:, a, kt, :], ada_g1[:, a, kt, :], col(4 * a + 1, kt),
                                         gamma(a, kt, 1), ALU.mult, ALU.add).then_inc(ada_step, 1)
            for a, kt in sets:
                dve.tensor_scalar(ada_scale[:, a, kt, :], ada_g1[:, a, kt, :], col(4 * a, kt), None, ALU.mult)\
                   .then_inc(ada_step, 1)
            dve.wait_ge(ada_step, 2 * len(sets))
            for a, kt in sets:
                dve.tensor_scalar(ada_shift[:, a, kt, :], ada_gb[:, a, kt, :], col(4 * a + 3, kt), None, ALU.add)\
                   .then_inc(ada_step, 1)

            def norm_rows(n):
                kind, b, _ = order[n]
                src, rows = source(n)
                if kind == C:
                    dve.wait_ge(ctx_loaded, 16 * (NB if b == NB - 1 else NB - 1))
                elif n < NB:
                    dve.wait_ge(x_in[b], 16)
                sublayer = sum(1 for other in order[:n] if other[0] == X) // NB
                if kind == X and sublayer > 0:
                    dve.wait_ge(o_added, 2 * (4 * (NP * sublayer - 1) + b) + 2)
                for tt in range(TT):
                    dve.bn_stats(stats[:, tt, :], src[:, tt, :]).then_inc(ln_step, 1)
                dve.wait_ge(ln_step, X_READ * n + TT)
                for tt in range(TT):
                    dve.bn_aggr(mean_var[:, tt, :], stats[:, tt, :]).then_inc(ln_step, 1)
                dve.wait_ge(ln_step, X_READ * n + 2 * TT)
                dve.tensor_scalar(var_eps[:, :], mean_var[:, :, 1], EPS, None, ALU.add).then_inc(ln_step, 1)
                at = X_READ * n + 2 * TT + 1
                dve.wait_ge(ln_step, at)
                dve.tensor_scalar(rstd[:, :].bitcast(I32), var_eps[:, :].bitcast(I32), -0.5, RSQRT_GUESS,
                                  ALU.mult, ALU.add).then_inc(ln_step, 1)
                for _ in range(NEWTON):
                    dve.wait_ge(ln_step, at + 1)
                    dve.tensor_tensor(newton[:, :], rstd[:, :], rstd[:, :], ALU.mult).then_inc(ln_step, 1)
                    dve.wait_ge(ln_step, at + 2)
                    dve.scalar_tensor_tensor(newton[:, :], newton[:, :], -0.5, var_eps[:, :], ALU.mult, ALU.mult)\
                       .then_inc(ln_step, 1)
                    dve.wait_ge(ln_step, at + 3)
                    dve.scalar_tensor_tensor(rstd[:, :], newton[:, :], 1.5, rstd[:, :], ALU.add, ALU.mult)\
                       .then_inc(ln_step, 1)
                    at += 3
                dve.wait_ge(ln_step, at + 1)
                for tt in range(TT):
                    dve.tensor_scalar(z[:, tt, 0:KT * rows], src[:, tt, :], mean_var[:, tt, 0:1],
                                      rstd[:, tt:tt + 1], ALU.subtract, ALU.mult).then_inc(ln_step, 1)

            def norm_split(n):
                kind, b, _ = order[n]
                rows = source(n)[1]
                hi, lo = (xn_hi, xn_lo) if kind == X else (ctx_hi, ctx_lo)
                for r in range(KT):
                    dve.wait_ge(ln_scaled, 2 * n + r + 1)
                    dve.tensor_copy(hi[0:rows, b, r, :], y[0:rows, :]).then_inc(ln_rounded, 1)
                    dve.wait_ge(ln_rounded, 2 * n + r + 1)
                    dve.tensor_tensor(lo[0:rows, b, r, :], y[0:rows, :], hi[0:rows, b, r, :], ALU.subtract)\
                       .then_inc(ln_split, 1)

            @there
            def rotate(x, tt):
                u = x[0]
                dve.wait_ge(v_ready, 4 * u + tt + 1)
                wait_for(dve, rot_ready, 4 * u + tt - 1)
                if isinstance(u, int) and u + tt == 0:
                    dve.wait_ge(rope_in, 16)
                qk = proj_ps[tt % 2][:, 0:2 * 128].rearrange("p (g d) -> p g d", g=4)
                dve.tensor_tensor(rot_a[:, tt % 2, :, :], qk, rope[:, 0, tt, :, :], ALU.mult)
                swapped = proj_ps[tt % 2][:, 0:2 * 128].rearrange("p (g s d) -> p g s d", g=4, s=2)[:, :, ::-1, :]
                dve.tensor_tensor(rot_b[:, tt % 2, :, :].rearrange("p g (s d) -> p g s d", s=2), swapped,
                                  rope[:, 1, tt, :, :].rearrange("p g (s d) -> p g s d", s=2), ALU.mult)\
                   .then_inc(roped, 1)

            @there
            def low(x, r):
                u, par, h = x[0], x[1] % 2, r // 2
                dve.wait_ge(qk_high, 4 * u + r + 1)
                if r % 2 == 0:
                    dve.tensor_tensor(q_lo[:, par, h, :], side_ps, q_hi[:, par, h, :], ALU.subtract)\
                       .then_inc(qk_low, 1)
                else:
                    k = k_parts[DH:128, par, h, :]
                    dve.tensor_tensor(k, side_ps[DH:128, :], k, ALU.subtract).then_inc(qk_low, 1)

            @there
            def peak(x, i):
                u, par = x[0], x[1] % 2
                dve.wait_ge(scored, 8 * u + i + 1)
                dve.tensor_reduce(neg_max[:, par, i:i + 1], ring_ps("S", i), AX.X, ALU.max, negate=True)\
                   .then_inc(maxed, 1)

            @there
            def invert(x, h):
                u, par = x[0], x[1] % 2
                dve.wait_ge(exped, 8 * u + TT * h + TT)
                cut = slice(TT * h, TT * h + TT)
                dve.reciprocal(row_inv[:, par, cut], row_sum[:, par, cut]).then_inc(inverted, 1)

            @there
            def normalise(x, i):
                u, par = x[0], x[1] % 2
                if i % TT == 0:
                    dve.wait_ge(inverted, 2 * u + i // TT + 1)
                dve.tensor_scalar(probs[:, i, :], probs[:, i, :], row_inv[:, par, i:i + 1], None, ALU.mult)\
                   .then_inc(normed, 1)

            @there
            def low_o(x):
                dve.wait_ge(o_high, x[0] + 1)
                dve.tensor_tensor(o_lo[:, :], av_ps, o_hi[:, :], ALU.subtract).then_inc(o_low, 1)

            @there
            def add_out(x_unit, r):
                u, b, _, phase = x_unit
                if r == 0:
                    dve.wait_ge(biased, NB * phase + b + 1)
                dve.wait_ge(o_projected, 2 * u + r + 1)
                rows = x[:, b, 2 * r:2 * r + 2, :]
                dve.tensor_tensor(rows, out_ps[r].rearrange("p (t d) -> p t d", d=D), rows, ALU.add)\
                   .then_inc(o_added, 1)

            def next_weights(w):
                dve.wait_ge(w_step, w + 1)
                dve.tensor_tensor(w_lo[:, :], w_raw[:, 0:WQKV], w_hi[:, :], ALU.subtract).then_inc(w_split, 1)

            @there
            def low_w(x):
                _, b, w, _ = x
                if b == NB - 1 and not (isinstance(w, int) and w == 2 * NP - 1):
                    next_weights(w + 1)

            def slot(w, b, now, nxt, later):
                peak(nxt, 0)
                normalise(now, 6)
                rotate(later, 0)
                normalise(now, 7)
                low(nxt, 2)
                peak(nxt, 1)
                rotate(later, 1)
                peak(nxt, 2)
                peak(nxt, 3)
                rotate(later, 2)
                low(nxt, 3)
                rotate(later, 3)
                low_w(later)
                invert(nxt, 0)
                peak(nxt, 4)
                peak(nxt, 5)
                normalise(nxt, 0)
                peak(nxt, 6)
                normalise(nxt, 1)
                normalise(nxt, 2)
                for n in mid_norm(w, b):
                    norm_split(n)
                if isinstance(w, int) and w == NP - 1:
                    norm_rows(norm_of(C, 0, b))
                low(later, 0)
                normalise(nxt, 3)
                peak(nxt, 7)
                low_o(now)
                low(later, 1)
                invert(nxt, 1)
                add_out(now, 0)
                normalise(nxt, 4)
                normalise(nxt, 5)
                add_out(now, 1)
                for n in end_norm(w, b):
                    norm_split(n)
                    if n + 1 < NB:
                        norm_rows(n + 1)
                for n in whole_norm(w, b):
                    norm_rows(n)
                if isinstance(w, int) and (w, b) == (2 * NP - 1, NB - 2):
                    dve.wait_ge(ffw_high, 1)
                    dve.tensor_tensor(w1_lo[:, :, :], w1_raw[:, :, :], w1_hi[:, :, :], ALU.subtract)\
                       .then_inc(ffw_split, 1)
                    dve.wait_ge(ffw_high, 2)
                    dve.tensor_tensor(w2_lo[:, :, :], w2_raw[:, :, :], w2_hi[:, :, :], ALU.subtract)\
                       .then_inc(ffw_split, 1)

            next_weights(0)
            norm_rows(0)
            norm_split(0)
            norm_rows(1)
            run_slots(dve, slot)
            norm_split(len(order) - 1)

            dve.wait_ge(biased, 3 * NB)
            with dve.Fori(0, NB) as b:
                for f in range(FT):
                    dve.wait_ge(hid_ready, 8 * b + f + 1)
                    if f >= 4:
                        dve.wait_ge(y_step, 8 * b + f - 3)
                    dve.tensor_copy(hid_hi[:, f % 4, :], hid[:, f % 4, :]).then_inc(hid_rounded, 1)
                    dve.wait_ge(hid_rounded, 8 * b + f + 1)
                    dve.tensor_tensor(hid_lo[:, f % 4, :], hid[:, f % 4, :], hid_hi[:, f % 4, :], ALU.subtract)\
                       .then_inc(hid_split, 1)
                dve.wait_ge(y_step, 8 * b + 8)
                rows = x[:, bass.ds(b, 1), :, :].rearrange("p a t d -> p (a t d)")
                dve.tensor_tensor(rows, ps[:, 4:6, :].rearrange("p a n -> p (a n)"), rows, ALU.add)\
                   .then_inc(y_added, 1)


def rotation_table():
    import numpy as np
    inv = np.float32(1.0) / np.float32(10000.0) ** (np.arange(0, DH, 2, dtype=np.float32) / np.float32(DH))
    angle = np.arange(N, dtype=np.float32)[:, None] * inv[None, :]
    cos, sin = np.cos(angle), np.sin(angle)
    both = np.stack([np.concatenate([cos, cos], 1), np.concatenate([-sin, sin], 1)])
    both = both.reshape(2, TT, 128, 1, DH).transpose(2, 0, 1, 3, 4)
    factor = np.array([DH ** -0.5] * 2 + [1.0] * 2, np.float32).reshape(1, 1, 1, 4, 1)
    return np.ascontiguousarray(both * factor, np.float32)


def kernel(**inputs):
    import numpy as np
    import concourse.bacc as bacc
    from concourse.bass_utils import run_bass_kernel_spmd

    def get(name):
        return np.asarray(inputs[name if name in inputs else "L0_xcond_" + name])

    def by_rows(a, tiles):
        return a.reshape(tiles, -1, a.shape[-1]).transpose(1, 0, 2)

    def pairs(a, apart):
        a = a.reshape(-1, NP, 2, DH // 2, 2) if apart else a.reshape(-1, NP, 2, 2, DH // 2)
        if apart:
            a = a.transpose(0, 1, 2, 4, 3)
        return a.reshape(-1, NP, 128).transpose(1, 0, 2)

    mid = H * DH
    pack = np.zeros((2 * NP, 128, WPACK), np.float32)
    for first, kind in ((0, "sa"), (NP, "ca")):
        wq, wkv, wo = get(kind + "_wq"), get(kind + "_wkv"), get(kind + "_wo")
        q, k, v = pairs(wq, True), pairs(wkv[:, :mid], True), pairs(wkv[:, mid:], False)
        for p in range(NP):
            if first == 0:
                qkv = by_rows(np.concatenate([q[p], k[p], v[p]], 1), KT)
                pack[p, :, 0:WQKV] = qkv.reshape(128, WQKV)
            else:
                pack[first + p, :, 0:KT * 128] = by_rows(q[p], KT).reshape(128, KT * 128)
                kv = by_rows(np.concatenate([k[p], v[p]], 1), KT)
                pack[first + p, 0:CK, KT * 128:WQKV] = kv.reshape(CK, KT * 256)
            pack[first + p, :, WQKV:WPACK] = wo[p * 128:(p + 1) * 128]
    columns = [get(n).reshape(KT, 128).T for n in
               ("ln1_w", "ln1_b", "g1_b", "b1_b", "ln2_w", "ln2_b", "g2_b", "b2_b")]
    columns.append(get("ff_b1").reshape(FT, 128).T)
    arrays = {
        "x_dram": get("x"),
        "ctx_dram": get("ctx_768"),
        "pack_dram": pack,
        "cond_dram": by_rows(get("cond_1024").T, KT),
        "ada_dram": np.stack([by_rows(get(n), KT) for n in ("g1_w", "b1_w", "g2_w", "b2_w")], 1),
        "cols_dram": np.concatenate(columns, 1),
        "ctxln_dram": np.stack([get(n).reshape(KT, CK).T for n in ("ca_lnc_w", "ca_lnc_b")], 1),
        "rows_dram": np.stack([get(n) for n in ("sa_bo", "ca_bo", "ff_b2")]),
        "w1_dram": by_rows(get("ff_w1"), KT),
        "w2_dram": by_rows(get("ff_w2"), FT),
        "rope_dram": rotation_table(),
    }
    arrays = {n: np.ascontiguousarray(a) for n, a in arrays.items()}
    nc = bacc.Bacc("TRN2", target_bir_lowering=False, num_devices=1)
    args = [nc.dram_tensor(n, a.shape, mybir.dt.from_np(a.dtype), kind="ExternalInput").ap()
            for n, a in arrays.items()]
    out = nc.dram_tensor("out", (NB, N, D), F32, kind="ExternalOutput").ap()
    build(nc, *args, out)
    return run_bass_kernel_spmd(nc, [arrays], core_ids=[0]).results[0]["out"]
```

```python
import concourse.bass as bass
from concourse import mybir
from contextlib import ExitStack

F32 = mybir.dt.float32
F32R = mybir.dt.float32r
I32 = mybir.dt.int32
ALU = mybir.AluOpType
ACT = mybir.ActivationFunctionType
AX = mybir.AxisListType

NB = 4
N = 512
TT = N // 128
D = 256
KT = D // 128
DC = 192
CK = DC // KT
DH = 64
H = 16
NP = H // 2
FF = 4 * D
FT = FF // 128
EPS = 1e-5
NEWTON = 3
RSQRT_GUESS = float(0x5F3759DF)
QKV = 3 * 128
WQKV = KT * QKV
WPACK = WQKV + D
T_BLOCKS = 2 * TT
S_TILES = 2 * TT
X_ROUNDS = 4
UNITS = NB * 2 * NP
RING = (("T", 2, 0), ("T", 3, 0), ("T", 4, 0), ("T", 5, 0), ("T", 6, 0), ("S", 0, 1),
        ("S", 1, 1), ("S", 2, 1), ("S", 3, 1), ("T", 7, 0), ("S", 4, 1), ("S", 5, 1),
        ("S", 6, 1), ("S", 7, 1), ("T", 0, 1), ("T", 1, 1))
SIDE = (("X", 1, 1), ("X", 2, 1), ("X", 3, 1), ("X", 0, 2), ("O", 1, 0))


def build(nc, x_d, ctx_d, pack_d, cond_d, ada_d, cols_d, ctxln_d, rows_d, w1_d, w2_d, rope_d, out_d):
    stack = ExitStack()
    with stack:
        attention_only = ExitStack()

        def sb(name, shape, dt=F32, where=stack):
            return where.enter_context(nc.sbuf_tensor(name, shape, dt))

        def sem(name):
            return stack.enter_context(nc.semaphore(name))

        x = sb("x", [128, NB, TT, D])
        xn_hi = sb("xn_hi", [128, NB, KT, N], F32R)
        xn_lo = sb("xn_lo", [128, NB, KT, N], F32R)
        ident = sb("ident", [128, 128])
        zero = sb("zero", [128, 1])
        cols = sb("cols", [128, 8 * KT + FT])
        cond = sb("cond", [128, KT, NB])
        ada_scale = sb("ada_scale", [128, 2, KT, NB])
        ada_shift = sb("ada_shift", [128, 2, KT, NB])
        ada_g1 = sb("ada_g1", [128, 2, KT, NB])
        ada_gb = sb("ada_gb", [128, 2, KT, NB])
        bias_rows = sb("bias_rows", [128, 3, D])
        stats = sb("stats", [128, TT, 6])
        mean_var = sb("mean_var", [128, TT, 2])
        rstd = sb("rstd", [128, TT])
        var_eps = sb("var_eps", [128, TT])
        newton = sb("newton", [128, TT])
        centre = sb("centre", [128, TT])
        z = sb("z", [128, TT, D])
        y = sb("y", [128, N])

        def asb(name, shape, dt=F32):
            return sb(name, shape, dt, attention_only)

        ctx_hi = asb("ctx_hi", [128, NB, KT, N], F32R)
        ctx_lo = asb("ctx_lo", [128, NB, KT, N], F32R)
        ctx_in = asb("ctx_rows", [128, NB - 1, TT, DC])
        ctx_ln = asb("ctx_ln", [CK, 2, KT])
        ada_w = asb("ada_w", [128, 4, KT, D])
        rope = asb("rope", [128, 2, TT, 4, DH])
        w_raw = asb("w_raw", [128, WPACK])
        w_hi = asb("w_hi", [128, WQKV], F32R)
        w_lo = asb("w_lo", [128, WQKV], F32R)
        wo_hi = asb("wo_hi", [128, D], F32R)
        wo_lo = asb("wo_lo", [128, D], F32R)
        rot_a = asb("rot_a", [128, 2, 4, DH])
        rot_b = asb("rot_b", [128, 2, 4, DH])
        rotated = asb("rotated", [128, TT, 4, 2, DH])
        q_hi = asb("q_hi", [128, 2, 2, N], F32R)
        q_lo = asb("q_lo", [128, 2, 2, N], F32R)
        k_parts = asb("k_parts", [128, 2, 2, N], F32R)
        v = asb("v", [128, NB, TT, 128])
        probs = asb("probs", [128, S_TILES, N])
        probs_t = asb("probs_t", [128, T_BLOCKS, N])
        neg_max = asb("neg_max", [128, 2, S_TILES])
        row_sum = asb("row_sum", [128, 2, S_TILES])
        row_inv = asb("row_inv", [128, 2, S_TILES])
        o_hi = asb("o_hi", [128, N], F32R)
        o_lo = asb("o_lo", [128, N], F32R)
        attention_only.close()

        w1_hi = sb("w1_hi", [128, KT, FF], F32R)
        w1_lo = sb("w1_lo", [128, KT, FF], F32R)
        w2_hi = sb("w2_hi", [128, FT, D], F32R)
        w2_lo = sb("w2_lo", [128, FT, D], F32R)
        w1_raw = sb("w1_raw", [128, KT, FF])
        w2_raw = sb("w2_raw", [128, FT, D])
        hid = sb("hid", [128, 4, N])
        hid_hi = sb("hid_hi", [128, 4, N], F32R)
        hid_lo = sb("hid_lo", [128, 4, N], F32R)

        ps = stack.enter_context(nc.psum_tensor("ps", [128, 8, N], F32))
        SIDE_AT = {(kind, n): pos for pos, (kind, n, _) in enumerate(SIDE)}
        RING_AT = {(kind, n): pos for pos, (kind, n, _) in enumerate(RING)}

        def ring_ps(kind, n):
            return ps[:, RING_AT[(kind, n)] % 4, :]

        av_ps = ps[:, 4, :]
        proj_ps = (ps[:, 5, :], ps[:, 7, :])
        side_ps = ps[:, 6, :]
        out_ps = (av_ps, side_ps)

        def norm_ps(n, r):
            return ((side_ps, proj_ps[1]) if n == 4 * NB - 1 else (av_ps, side_ps))[r]

        ada_in = sem("ada_in")
        ada2_in = sem("ada2_in")
        cols_in = sem("cols_in")
        rope_in = sem("rope_in")
        rows_in = sem("rows_in")
        x_in = [sem(f"x_in{b}") for b in range(NB)]
        ctx_loaded = sem("ctx_loaded")
        ident_ready = sem("ident_ready")
        zero_ready = sem("zero_ready")
        ada_mm = sem("ada_mm")
        ada_step = sem("ada_step")
        ln_step = sem("ln_step")
        ln_newton = sem("ln_newton")
        ln_rows = sem("ln_rows")
        ln_turned = sem("ln_turned")
        ln_scaled = sem("ln_scaled")
        ln_split = sem("ln_split")
        biased = sem("biased")
        w_loaded = sem("w_loaded")
        w_step = sem("w_step")
        w_split = sem("w_split")
        wo_step = sem("wo_step")
        wo_split = sem("wo_split")
        projected = sem("projected")
        roped = sem("roped")
        v_ready = sem("v_ready")
        rot_ready = sem("rot_ready")
        qk_turned = sem("qk_turned")
        qk_high = sem("qk_high")
        qk_low = sem("qk_low")
        scored = sem("scored")
        maxed = sem("maxed")
        exped = sem("exped")
        inverted = sem("inverted")
        normed = sem("normed")
        last_normed = sem("last_normed")
        turned = sem("turned")
        probs_t_ready = sem("probs_t_ready")
        averaged = sem("averaged")
        o_high = sem("o_high")
        o_low = sem("o_low")
        o_projected = sem("o_projected")
        o_added = sem("o_added")
        ffw_loaded = sem("ffw_loaded")
        ffw_high = sem("ffw_high")
        ffw_split = sem("ffw_split")
        hid_mm = sem("hid_mm")
        hid_ready = sem("hid_ready")
        hid_rounded = sem("hid_rounded")
        hid_split = sem("hid_split")
        y_step = sem("y_step")
        y_added = sem("y_added")
        stored = sem("stored")

        X, C = 0, 1
        order = [(X, b, 0) for b in range(NB)]
        order += [(C, b, 0) for b in range(NB)]
        order += [(X, b, 0) for b in range(NB)]
        order += [(X, b, 1) for b in range(NB)]

        def norm_of(kind, sublayer, b):
            return NB + b if kind == C else (b, 2 * NB + b, 3 * NB + b)[sublayer]

        STATS = 2 * TT + 2
        STEPS = 4 * NEWTON + 2

        def invert_root(eng, n):
            eng.wait_ge(ln_step, STATS * (n + 1))
            at = STEPS * n
            for k in range(NEWTON):
                if k > 0:
                    eng.wait_ge(ln_newton, at)
                eng.tensor_tensor(newton[:, :], rstd[:, :], rstd[:, :], ALU.mult).then_inc(ln_newton, 1)
                eng.wait_ge(ln_newton, at + 1)
                eng.tensor_tensor(newton[:, :], newton[:, :], var_eps[:, :], ALU.mult).then_inc(ln_newton, 1)
                eng.wait_ge(ln_newton, at + 2)
                eng.tensor_scalar(newton[:, :], newton[:, :], -0.5, 1.5, ALU.mult, ALU.add).then_inc(ln_newton, 1)
                eng.wait_ge(ln_newton, at + 3)
                eng.tensor_tensor(rstd[:, :], newton[:, :], rstd[:, :], ALU.mult).then_inc(ln_newton, 1)
                at += 4
            eng.wait_ge(ln_newton, at)
            eng.tensor_tensor(newton[:, :], mean_var[:, :, 0], rstd[:, :], ALU.mult).then_inc(ln_newton, 1)
            eng.wait_ge(ln_newton, at + 1)
            eng.tensor_scalar(centre[:, :], newton[:, :], -1.0, None, ALU.mult).then_inc(ln_newton, 1)

        def unit(w, b, phase, ahead):
            b += ahead
            if b >= NB:
                w, b = w + 1, b - NB
            if isinstance(w, int):
                if not 0 <= w < 2 * NP:
                    return None
                phase = w // NP
            return 4 * w + b, b, w, phase

        def run_slots(eng, slot):
            def step(w, phase, batches=range(NB)):
                for b in batches:
                    slot(w, b, unit(w, b, phase, 0), unit(w, b, phase, 1), unit(w, b, phase, 2))

            step(-1, 0, range(NB - 2, NB))
            for phase in range(2):
                first = phase * NP
                step(first, phase)
                with eng.Fori(first + 1, first + NP - 1) as w:
                    step(w, phase)
                step(first + NP - 1, phase)

        def there(step):
            return lambda x, *which: step(x, *which) if x is not None else None

        def wait_for(eng, signal, count):
            if not (isinstance(count, int) and count <= 0):
                eng.wait_ge(signal, count)

        def prior(uses, pos, u):
            stride = 4 if uses is RING else 1
            for back in range(stride, 3 * len(uses), stride):
                slots_back, at = divmod(pos - back, len(uses))
                kind, n, ahead = uses[at]
                v = u + (slots_back + ahead)
                if not isinstance(v, int) or 0 <= v < UNITS:
                    return kind, n, v
            return None

        LAST = len(order) - 1
        stats_at_end_of = {u: u + 4 for u in range(-2, NB)}
        turned_in_slot = {u: u + 3 for u in range(-2, NB)}
        turned_in_slot[NB * (NP - 1)] = norm_of(C, 0, NB - 1)
        for sublayer in (1, 2):
            for b in range(NB):
                u = NB * (NP * sublayer - 1) + b
                stats_at_end_of[u] = norm_of(X, sublayer, b)
                turned_in_slot[u + 1] = norm_of(X, sublayer, b)
        del turned_in_slot[UNITS]

        def of_slot(table, w, b):
            return [table[NB * w + b]] if isinstance(w, int) and NB * w + b in table else []

        def stats_at_end(w, b):
            return of_slot(stats_at_end_of, w, b)

        def turned_in(w, b):
            return of_slot(turned_in_slot, w, b)

        def source(n):
            kind, b, _ = order[n]
            return (x[:, b, :, :], 128) if kind == X else (ctx_in[:, b % (NB - 1), :, :], CK)

        ADA_STEPS = 4 * KT
        block = stack.enter_context(nc.Block())

        @block.sync
        def _(sp):
            sp.dma_start(x[:, 0, :, :], x_d[0].rearrange("(t p) d -> p t d", p=128)).then_inc(x_in[0], 16)
            sp.dma_start(w_raw[:, :], pack_d[0]).then_inc(w_loaded, 16)
            for b in range(1, NB):
                sp.dma_start(x[:, b, :, :], x_d[b].rearrange("(t p) d -> p t d", p=128)).then_inc(x_in[b], 16)
            for b in range(NB - 1):
                sp.dma_start(ctx_in[:, b, :, :], ctx_d[b].rearrange("(t p) d -> p t d", p=128))\
                  .then_inc(ctx_loaded, 16)

            def next_pair(w):
                sp.wait_ge(w_split, w)
                sp.wait_ge(wo_split, w)
                sp.dma_start(w_raw[:, :], pack_d[bass.ds(w, 1), :, :].rearrange("a p c -> p (a c)"))\
                  .then_inc(w_loaded, 16)

            next_pair(1)
            sp.wait_ge(ln_split, 2 * norm_of(C, 0, 0) + 2)
            sp.dma_start(ctx_in[:, 0, :, :], ctx_d[NB - 1].rearrange("(t p) d -> p t d", p=128))\
              .then_inc(ctx_loaded, 16)
            with sp.Fori(2, 2 * NP) as w:
                next_pair(w)
            sp.wait_ge(ln_split, 2 * norm_of(C, 0, NB - 1) + 2)
            sp.dma_start(w1_raw[:, :, :], w1_d).then_inc(ffw_loaded, 16)
            sp.dma_start(w2_raw[:, :, :], w2_d).then_inc(ffw_loaded, 16)
            with sp.Fori(0, NB) as b:
                sp.wait_ge(y_added, b + 1)
                sp.dma_start(out_d[bass.ds(b, 1), :, :].rearrange("a (t p) d -> p (a t) d", p=128),
                             x[:, bass.ds(b, 1), :, :].rearrange("p a t d -> p (a t) d")).then_inc(stored, 16)
            sp.wait_ge(stored, 16 * NB)

        @block.gpsimd
        def _(pool):
            pool.memset(ident[:, :], 0.0).then_inc(ident_ready, 1)
            pool.memset(zero[:, :], 0.0).then_inc(zero_ready, 1)
            pool.wait_ge(ident_ready, 1)
            pool.affine_select(out=ident[:, :], in_=ident[:, :], compare_op=ALU.not_equal, fill=1.0,
                               base=0, pattern=[[-1, 128]], channel_multiplier=1).then_inc(ident_ready, 1)

            @there
            def split_wo(x):
                u, b, w, _ = x
                if b > 0:
                    return
                raw = w_raw[:, WQKV:WPACK]
                pool.wait_ge(w_loaded, 16 * w + 16)
                wait_for(pool, o_projected, 2 * u)
                pool.tensor_tensor(wo_hi[:, :], raw, zero[:, :].broadcast_to([128, D]), ALU.add).then_inc(wo_step, 1)
                pool.wait_ge(wo_step, w + 1)
                pool.tensor_tensor(wo_lo[:, :], raw, wo_hi[:, :], ALU.subtract)\
                    .then_inc(wo_split, 1)

            @there
            def add_rotation(x, tt):
                u = x[0]
                pool.wait_ge(roped, 4 * u + tt + 1)
                if tt == 0:
                    wait_for(pool, qk_turned, 4 * u)
                a = rot_a[:, tt % 2, :, :].unsqueeze(2).broadcast_to([128, 4, 2, DH])
                c = rot_b[:, tt % 2, :, :].unsqueeze(2).broadcast_to([128, 4, 2, DH])
                pool.tensor_tensor(rotated[:, tt, :, :, :], a, c, ALU.add).then_inc(rot_ready, 1)

            def add_bias(n):
                b = order[n][1]
                sublayer = sum(1 for kind, _, _ in order[:n] if kind == X) // NB
                pool.wait_ge(ln_rows, TT * (n + 1))
                pool.tensor_tensor(x[:, b, :, :], x[:, b, :, :],
                                   bias_rows[:, sublayer, :].unsqueeze(1).broadcast_to([128, TT, D]),
                                   ALU.add).then_inc(biased, 1)

            def split_ffw(raw, hi, lo, width, nth):
                pool.tensor_tensor(hi[:, :, :], raw[:, :, :],
                                   zero[:, :].unsqueeze(2).broadcast_to([128, KT * FF // width, width]),
                                   ALU.add).then_inc(ffw_high, 1)
                pool.wait_ge(ffw_high, nth)
                pool.tensor_tensor(lo[:, :, :], raw[:, :, :], hi[:, :, :], ALU.subtract).then_inc(ffw_split, 1)

            def slot(w, b, now, nxt, later):
                split_wo(now)
                add_rotation(later, 0)
                add_rotation(later, 1)
                for n in turned_in(w, b):
                    if order[n][0] == X:
                        add_bias(n)
                add_rotation(later, 2)
                add_rotation(later, 3)
                if isinstance(w, int) and (w, b) == (2 * NP - 1, NB - 2):
                    pool.wait_ge(projected, 4 * UNITS)
                    pool.wait_ge(ffw_loaded, 32)
                    split_ffw(w1_raw, w1_hi, w1_lo, FF, 1)
                if isinstance(w, int) and (w, b) == (2 * NP - 1, NB - 1):
                    split_ffw(w2_raw, w2_hi, w2_lo, D, 2)
                for n in stats_at_end(w, b):
                    invert_root(pool, n)

            pool.wait_ge(zero_ready, 1)
            invert_root(pool, 1)
            pool.wait_ge(rows_in, 16)
            add_bias(0)
            run_slots(pool, slot)
            add_bias(LAST)

        @block.scalar
        def _(act):
            act.dma_start(cond[:, :, :], cond_d).then_inc(ada_in, 16)
            act.dma_start(ada_w[:, 0:2, :, :], ada_d[:, 0:2]).then_inc(ada_in, 16)
            act.dma_start(ada_w[:, 2:4, :, :], ada_d[:, 2:4]).then_inc(ada2_in, 16)
            act.dma_start(cols[:, :], cols_d).then_inc(cols_in, 16)
            act.dma_start(ctx_ln[:, :, :], ctxln_d).then_inc(cols_in, 16)
            act.dma_start(rope[:, :, :, :, :], rope_d).then_inc(rope_in, 16)
            act.dma_start(bias_rows[:, :, :], rows_d.partition_broadcast(128)).then_inc(rows_in, 16)

            def norm_rows(n):
                src, rows = source(n)
                act.wait_ge(ln_newton, STEPS * (n + 1))
                if n > 0:
                    act.wait_ge(ln_turned, 2 * n)
                for tt in range(TT):
                    act.activation(z[:, tt, 0:KT * rows], src[:, tt, :], ACT.Identity, bias=centre[:, tt:tt + 1],
                                   scale=rstd[:, tt:tt + 1]).then_inc(ln_rows, 1)

            def norm(n, r):
                kind, b, ada = order[n]
                rows = source(n)[1]
                act.wait_ge(ln_turned, 2 * n + r + 1)
                if 2 * n + r > 0:
                    act.wait_ge(ln_split, 2 * n + r)
                if kind == X:
                    scale, shift = ada_scale[:, ada, r, b:b + 1], ada_shift[:, ada, r, b:b + 1]
                else:
                    scale, shift = ctx_ln[:, 0, r:r + 1], ctx_ln[:, 1, r:r + 1]
                hi = (xn_hi if kind == X else ctx_hi)[0:rows, b, r, :]
                turned_rows = norm_ps(n, r)[0:rows, :]
                act.activation(y[0:rows, :], turned_rows, ACT.Identity, bias=shift, scale=scale)
                act.activation(hi, turned_rows, ACT.Identity, bias=shift, scale=scale).then_inc(ln_scaled, 1)

            @there
            def keep_v(x, tt):
                u, b = x[:2]
                act.wait_ge(projected, 4 * u + tt + 1)
                act.copy(v[:, b, tt, :], proj_ps[tt % 2][:, 2 * 128:QKV]).then_inc(v_ready, 1)

            @there
            def high(x, r):
                u, b = x[:2]
                act.wait_ge(qk_turned, 4 * u + r + 1)
                dst = (k_parts if r % 2 else q_hi)[:, b % 2, r // 2, :]
                act.copy(dst, side_ps).then_inc(qk_high, 1)

            @there
            def exp(x, i):
                u, par = x[0], x[1] % 2
                act.wait_ge(maxed, 8 * u + i + 1)
                if i % TT == 0:
                    wait_for(act, turned, 8 * u - 8 + i + TT)
                act.activation(probs[:, i, :], ring_ps("S", i), ACT.Exp, bias=neg_max[:, par, i:i + 1],
                               accum_out=row_sum[:, par, i:i + 1]).then_inc(exped, 1)

            @there
            def normalise_last(x, h):
                u, par = x[0], x[1] % 2
                t = TT * h + TT - 1
                act.wait_ge(inverted, 2 * u + h + 1)
                act.activation(probs[:, t, :], probs[:, t, :], ACT.Identity, bias=zero[:, :],
                               scale=row_inv[:, par, t:t + 1]).then_inc(last_normed, 1)

            @there
            def keep_turned(x, j):
                u = x[0]
                act.wait_ge(turned, 8 * u + j + 1)
                if j < TT:
                    wait_for(act, averaged, 4 * u - 4 + j + 1)
                act.copy(probs_t[:, j, :], ring_ps("T", j)).then_inc(probs_t_ready, 1)

            @there
            def high_o(x):
                act.wait_ge(averaged, 4 * x[0] + 4)
                act.copy(o_hi[:, :], av_ps).then_inc(o_high, 1)

            def next_weights(w):
                act.wait_ge(w_loaded, 16 * w + 16)
                act.copy(w_hi[:, :], w_raw[:, 0:WQKV]).then_inc(w_step, 1)

            @there
            def round_w(x):
                u, b, w, _ = x
                if b == NB - 1 and not (isinstance(w, int) and w == 2 * NP - 1):
                    act.wait_ge(projected, 4 * u + 4)
                    next_weights(w + 1)

            def slot(w, b, now, nxt, later):
                keep_turned(now, 1)
                normalise_last(now, 1)
                high(nxt, 1)
                keep_v(later, 0)
                keep_turned(now, 2)
                keep_v(later, 1)
                keep_turned(now, 3)
                keep_turned(now, 4)
                keep_turned(now, 5)
                high(nxt, 2)
                keep_turned(now, 6)
                for n in turned_in(w, b):
                    norm_rows(n)
                keep_v(later, 2)
                exp(nxt, 0)
                high(nxt, 3)
                exp(nxt, 1)
                for n in turned_in(w, b):
                    norm(n, 0)
                keep_v(later, 3)
                exp(nxt, 2)
                round_w(later)
                exp(nxt, 3)
                keep_turned(now, 7)
                for n in turned_in(w, b):
                    norm(n, 1)
                exp(nxt, 4)
                high_o(now)
                normalise_last(nxt, 0)
                high(later, 0)
                exp(nxt, 5)
                keep_turned(nxt, 0)
                exp(nxt, 6)
                exp(nxt, 7)

            next_weights(0)
            norm_rows(0)
            act.wait_ge(cols_in, 32)
            act.wait_ge(ada_step, ADA_STEPS)
            norm(0, 0)
            norm(0, 1)
            act.wait_ge(zero_ready, 1)
            run_slots(act, slot)

            def mlp(b):
                for f in range(FT):
                    act.wait_ge(hid_mm, 8 * b + f + 1)
                    if f >= 4:
                        act.wait_ge(hid_split, 8 * b + f - 3)
                    act.activation(hid[:, f % 4, :], ps[:, f % 4, :], ACT.Gelu,
                                   bias=cols[:, 8 * KT + f:8 * KT + f + 1]).then_inc(hid_ready, 1)

            mlp(0)
            norm_rows(LAST)
            norm(LAST, 0)
            norm(LAST, 1)
            with act.Fori(1, NB) as b:
                mlp(b)

        @block.tensor
        def _(pe):
            def modulate(a):
                pe.wait_ge(*((ada_in, 32), (ada2_in, 16))[a])
                for m in (2 * a, 2 * a + 1):
                    for kt in range(KT):
                        for kc in range(KT):
                            mm = pe.matmul(ps[:, a, (m * KT + kt) * NB:(m * KT + kt + 1) * NB],
                                           ada_w[:, m, kc, kt * 128:(kt + 1) * 128], cond[:, kc, :],
                                           start=(kc == 0), stop=(kc == KT - 1))
                mm.then_inc(ada_mm, 1)

            modulate(0)
            pe.wait_ge(ident_ready, 2)

            def parts(out, a_hi, a_lo, b_hi, b_lo, first=True, last=True):
                pe.matmul(out, a_hi, b_hi, start=first, stop=False)
                pe.matmul(out, a_hi, b_lo, start=False, stop=False)
                return pe.matmul(out, a_lo, b_hi, start=False, stop=last)

            def norm(n, r):
                rows = source(n)[1]
                pe.wait_ge(ln_rows, TT * (n + 1))
                for tt in range(TT):
                    mm = pe.transpose(norm_ps(n, r)[0:rows, tt * 128:(tt + 1) * 128],
                                      z[:, tt, r * rows:(r + 1) * rows], ident[:, :])
                mm.then_inc(ln_turned, 1)

            @there
            def project(x, tt):
                u, b, w, phase = x
                cut = slice(tt * 128, (tt + 1) * 128)
                if tt == 0:
                    pe.wait_ge(ln_split, 2 * norm_of(X, phase, b) + 2)
                    pe.wait_ge(w_split, w + 1)
                wait_for(pe, roped, 4 * u + tt - 1)
                out = proj_ps[tt % 2]
                if phase == 0:
                    for kt in range(KT):
                        c = slice(kt * QKV, (kt + 1) * QKV)
                        mm = parts(out[:, 0:QKV], xn_hi[:, b, kt, cut], xn_lo[:, b, kt, cut],
                                   w_hi[:, c], w_lo[:, c], kt == 0, kt == KT - 1)
                else:
                    if tt == 0:
                        pe.wait_ge(ln_split, 2 * norm_of(C, 0, b) + 2)
                    for kt in range(KT):
                        c = slice(kt * 128, (kt + 1) * 128)
                        parts(out[:, 0:128], xn_hi[:, b, kt, cut], xn_lo[:, b, kt, cut],
                              w_hi[:, c], w_lo[:, c], kt == 0, kt == KT - 1)
                    for kt in range(KT):
                        c = slice(KT * 128 + kt * 256, KT * 128 + (kt + 1) * 256)
                        mm = parts(out[:, 128:QKV], ctx_hi[0:CK, b, kt, cut], ctx_lo[0:CK, b, kt, cut],
                                   w_hi[0:CK, c], w_lo[0:CK, c], kt == 0, kt == KT - 1)
                mm.then_inc(projected, 1)

            def claim_side(pos, u):
                before = prior(SIDE, pos, u)
                if before is not None:
                    kind, n, v = before
                    if kind == "X":
                        wait_for(pe, qk_low, 4 * v + n + 1)
                    else:
                        wait_for(pe, o_added, 2 * v + 2)

            @there
            def turn_qk(x, r):
                u = x[0]
                if r == 0:
                    pe.wait_ge(rot_ready, 4 * u + 4)
                pos = SIDE_AT[("X", r)]
                claim_side(pos, u - SIDE[pos][2])
                for tt in range(TT):
                    mm = pe.transpose(side_ps[:, tt * 128:(tt + 1) * 128],
                                      rotated[:, tt, 2 * (r % 2) + r // 2, :, :].rearrange("p a d -> p (a d)"),
                                      ident[:, :])
                mm.then_inc(qk_turned, 1)

            def claim(kind, n, u):
                pos = RING_AT[(kind, n)]
                before = prior(RING, pos, u - RING[pos][2])
                if before is not None:
                    was, m, v = before
                    wait_for(pe, exped if was == "S" else probs_t_ready, 8 * v + m + 1)
                return ps[:, pos % 4, :]

            @there
            def score(x, i):
                u, par = x[0], x[1] % 2
                h, cut = i // TT, slice(i % TT * 128, (i % TT + 1) * 128)
                if i % TT == 0:
                    pe.wait_ge(qk_low, 4 * u + 2 * h + 2)
                bank = claim("S", i, u)
                pe.matmul(bank, q_hi[:, par, h, cut], k_parts[:, par, h, :], start=True, stop=False)
                pe.matmul(bank, q_lo[:, par, h, cut], k_parts[:, par, h, :], start=False, stop=True)\
                  .then_inc(scored, 1)

            @there
            def turn_probs(x, j):
                u = x[0]
                h, kt = divmod(j, TT)
                if kt == 0:
                    pe.wait_ge(normed, 6 * u + 3 * h + 3)
                    pe.wait_ge(last_normed, 2 * u + h + 1)
                bank = claim("T", j, u)
                for qt in range(TT):
                    mm = pe.transpose(bank[:, qt * 128:(qt + 1) * 128],
                                      probs[:, TT * h + qt, kt * 128:(kt + 1) * 128], ident[:, :])
                mm.then_inc(turned, 1)

            @there
            def average(x, kt):
                u, b = x[:2]
                if kt == 0:
                    pe.wait_ge(v_ready, 4 * u + 4)
                    wait_for(pe, o_added, 2 * u - 1)
                pe.wait_ge(probs_t_ready, 8 * u + TT + kt + 1)
                for h in range(2):
                    mm = pe.matmul(av_ps[DH * h:DH * h + DH, :], v[:, b, kt, DH * h:DH * h + DH],
                                   probs_t[:, TT * h + kt, :], start=(kt == 0), stop=(kt == TT - 1))
                mm.then_inc(averaged, 1)

            @there
            def project_out(x, r):
                u, _, w, _ = x
                if r == 0:
                    pe.wait_ge(o_low, u + 1)
                    pe.wait_ge(wo_split, w + 1)
                else:
                    claim_side(SIDE_AT[("O", r)], u)
                for t in range(2):
                    cut = slice((2 * r + t) * 128, (2 * r + t + 1) * 128)
                    mm = parts(out_ps[r][:, t * D:(t + 1) * D], o_hi[:, cut], o_lo[:, cut], wo_hi[:, :], wo_lo[:, :])
                mm.then_inc(o_projected, 1)

            def slot(w, b, now, nxt, later):
                project(later, 0)
                turn_probs(now, 2)
                turn_qk(nxt, 1)
                project(later, 1)
                turn_probs(now, 3)
                turn_probs(now, 4)
                turn_probs(now, 5)
                turn_qk(nxt, 2)
                turn_probs(now, 6)
                score(nxt, 0)
                project(later, 2)
                score(nxt, 1)
                turn_qk(nxt, 3)
                score(nxt, 2)
                score(nxt, 3)
                for n in turned_in(w, b):
                    wait_for(pe, o_added, 2 * (NB * w + b) - 1)
                    norm(n, 0)
                project(later, 3)
                turn_probs(now, 7)
                for n in turned_in(w, b):
                    claim_side(SIDE_AT[("X", 3)] + 1, NB * w + b)
                    norm(n, 1)
                score(nxt, 4)
                for n in turned_in(w, b):
                    pe.wait_ge(ln_scaled, 2 * n + 1)
                average(now, 0)
                average(now, 1)
                average(now, 2)
                average(now, 3)
                score(nxt, 5)
                for n in turned_in(w, b):
                    pe.wait_ge(ln_scaled, 2 * n + 2)
                turn_qk(later, 0)
                score(nxt, 6)
                score(nxt, 7)
                turn_probs(nxt, 0)
                project_out(now, 0)
                turn_probs(nxt, 1)
                project_out(now, 1)

            norm(0, 0)
            norm(0, 1)
            modulate(1)
            pe.wait_ge(ln_scaled, 2)
            run_slots(pe, slot)

            pe.wait_ge(ffw_split, 1)

            def mlp(b):
                pe.wait_ge(ln_split, 2 * (norm_of(X, 2, 0) + b) + 2)

                def hidden(f):
                    if f >= 4:
                        pe.wait_ge(hid_ready, 8 * b + f - 3)
                    cut = slice(f * 128, (f + 1) * 128)
                    for kt in range(KT):
                        hi = xn_hi[:, bass.ds(b, 1), kt, :].rearrange("p a n -> p (a n)")
                        lo = xn_lo[:, bass.ds(b, 1), kt, :].rearrange("p a n -> p (a n)")
                        mm = parts(ps[:, f % 4, :], w1_hi[:, kt, cut], w1_lo[:, kt, cut], hi, lo,
                                   kt == 0, kt == KT - 1)
                    mm.then_inc(hid_mm, 1)

                def down(f):
                    pe.wait_ge(hid_split, 8 * b + f + 1)
                    for tt in range(TT):
                        out = ps[:, 4 + tt // 2, tt % 2 * D:(tt % 2 + 1) * D]
                        cut = slice(tt * 128, (tt + 1) * 128)
                        hi, lo = hid_hi[:, f % 4, cut], hid_lo[:, f % 4, cut]
                        for n, (a, c) in enumerate(((hi, w2_hi), (hi, w2_lo), (lo, w2_hi))):
                            mm = pe.matmul(out, a, c[:, f, :], start=(f == 0 and n == 0 and tt % 2 == 0),
                                           stop=(f == FT - 1 and n == 2), skip_group_check=True)
                    mm.then_inc(y_step, 1)

                for f in range(3):
                    hidden(f)
                pe.wait_ge(ffw_split, 2)
                for f in range(FT):
                    if f + 3 < FT:
                        hidden(f + 3)
                    down(f)

            mlp(0)
            norm(LAST, 0)
            norm(LAST, 1)
            with pe.Fori(1, NB) as b:
                mlp(b)

        @block.vector
        def _(dve):
            def gamma(a, kt, beta=0):
                at = ((2 * a + beta) * KT + kt) * NB
                return ps[:, a, at:at + NB]

            def col(j, kt):
                return cols[:, j * KT + kt:j * KT + kt + 1]

            def modulate(a):
                dve.wait_ge(ada_mm, a + 1)
                dve.wait_ge(cols_in, 32)
                for kt in range(KT):
                    dve.tensor_scalar(ada_g1[:, a, kt, :], gamma(a, kt), col(4 * a + 2, kt), 1.0, ALU.add, ALU.add)\
                       .then_inc(ada_step, 1)
                at = 4 * KT * a + KT
                dve.wait_ge(ada_step, at)
                for kt in range(KT):
                    dve.scalar_tensor_tensor(ada_gb[:, a, kt, :], ada_g1[:, a, kt, :], col(4 * a + 1, kt),
                                             gamma(a, kt, 1), ALU.mult, ALU.add).then_inc(ada_step, 1)
                for kt in range(KT):
                    dve.tensor_scalar(ada_scale[:, a, kt, :], ada_g1[:, a, kt, :], col(4 * a, kt), None, ALU.mult)\
                       .then_inc(ada_step, 1)
                dve.wait_ge(ada_step, at + 2 * KT)
                for kt in range(KT):
                    dve.tensor_scalar(ada_shift[:, a, kt, :], ada_gb[:, a, kt, :], col(4 * a + 3, kt), None, ALU.add)\
                       .then_inc(ada_step, 1)

            def norm_stats(n):
                kind, b, _ = order[n]
                src = source(n)[0]
                if kind == C:
                    dve.wait_ge(ctx_loaded, 16 * (NB if b == NB - 1 else NB - 1))
                elif n < NB:
                    dve.wait_ge(x_in[b], 16)
                else:
                    sublayer = (n - NB) // NB
                    dve.wait_ge(o_added, 2 * (4 * (NP * sublayer - 1) + b) + 2)
                for tt in range(TT):
                    dve.bn_stats(stats[:, tt, :], src[:, tt, :]).then_inc(ln_step, 1)
                dve.wait_ge(ln_step, STATS * n + TT)
                if n > 0:
                    dve.wait_ge(ln_rows, TT * n)
                for tt in range(TT):
                    dve.bn_aggr(mean_var[:, tt, :], stats[:, tt, :]).then_inc(ln_step, 1)
                dve.wait_ge(ln_step, STATS * n + 2 * TT)
                dve.tensor_scalar(var_eps[:, :], mean_var[:, :, 1], EPS, None, ALU.add).then_inc(ln_step, 1)
                dve.wait_ge(ln_step, STATS * n + 2 * TT + 1)
                dve.tensor_scalar(rstd[:, :].bitcast(I32), var_eps[:, :].bitcast(I32), -0.5, RSQRT_GUESS,
                                  ALU.mult, ALU.add).then_inc(ln_step, 1)

            def norm_split(n, r):
                kind, b, _ = order[n]
                rows = source(n)[1]
                hi, lo = (xn_hi, xn_lo) if kind == X else (ctx_hi, ctx_lo)
                dve.wait_ge(ln_scaled, 2 * n + r + 1)
                dve.tensor_tensor(lo[0:rows, b, r, :], y[0:rows, :], hi[0:rows, b, r, :], ALU.subtract)\
                   .then_inc(ln_split, 1)

            @there
            def rotate(x, tt):
                u = x[0]
                dve.wait_ge(v_ready, 4 * u + tt + 1)
                wait_for(dve, rot_ready, 4 * u + tt - 1)
                if isinstance(u, int) and u + tt == 0:
                    dve.wait_ge(rope_in, 16)
                qk = proj_ps[tt % 2][:, 0:2 * 128].rearrange("p (g d) -> p g d", g=4)
                dve.tensor_tensor(rot_a[:, tt % 2, :, :], qk, rope[:, 0, tt, :, :], ALU.mult)
                swapped = proj_ps[tt % 2][:, 0:2 * 128].rearrange("p (g s d) -> p g s d", g=4, s=2)[:, :, ::-1, :]
                dve.tensor_tensor(rot_b[:, tt % 2, :, :].rearrange("p g (s d) -> p g s d", s=2), swapped,
                                  rope[:, 1, tt, :, :].rearrange("p g (s d) -> p g s d", s=2), ALU.mult)\
                   .then_inc(roped, 1)

            @there
            def low(x, r):
                u, par, h = x[0], x[1] % 2, r // 2
                dve.wait_ge(qk_high, 4 * u + r + 1)
                if r % 2 == 0:
                    dve.tensor_tensor(q_lo[:, par, h, :], side_ps, q_hi[:, par, h, :], ALU.subtract)\
                       .then_inc(qk_low, 1)
                else:
                    k = k_parts[DH:128, par, h, :]
                    dve.tensor_tensor(k, side_ps[DH:128, :], k, ALU.subtract).then_inc(qk_low, 1)

            @there
            def peak(x, i):
                u, par = x[0], x[1] % 2
                dve.wait_ge(scored, 8 * u + i + 1)
                dve.tensor_reduce(neg_max[:, par, i:i + 1], ring_ps("S", i), AX.X, ALU.max, negate=True)\
                   .then_inc(maxed, 1)

            @there
            def invert(x, h):
                u, par = x[0], x[1] % 2
                dve.wait_ge(exped, 8 * u + TT * h + TT)
                cut = slice(TT * h, TT * h + TT)
                dve.reciprocal(row_inv[:, par, cut], row_sum[:, par, cut]).then_inc(inverted, 1)

            @there
            def normalise(x, i):
                u, par = x[0], x[1] % 2
                h, t = divmod(i, TT - 1)
                if t == 0:
                    dve.wait_ge(inverted, 2 * u + h + 1)
                t += TT * h
                dve.tensor_scalar(probs[:, t, :], probs[:, t, :], row_inv[:, par, t:t + 1], None, ALU.mult)\
                   .then_inc(normed, 1)

            @there
            def low_o(x):
                dve.wait_ge(o_high, x[0] + 1)
                dve.tensor_tensor(o_lo[:, :], av_ps, o_hi[:, :], ALU.subtract).then_inc(o_low, 1)

            @there
            def add_out(x_unit, r):
                u, b, _, phase = x_unit
                if r == 0:
                    dve.wait_ge(biased, NB * phase + b + 1)
                dve.wait_ge(o_projected, 2 * u + r + 1)
                rows = x[:, b, 2 * r:2 * r + 2, :]
                dve.tensor_tensor(rows, out_ps[r].rearrange("p (t d) -> p t d", d=D), rows, ALU.add)\
                   .then_inc(o_added, 1)

            def next_weights(w):
                dve.wait_ge(w_step, w + 1)
                dve.tensor_tensor(w_lo[:, :], w_raw[:, 0:WQKV], w_hi[:, :], ALU.subtract).then_inc(w_split, 1)

            @there
            def low_w(x):
                _, b, w, _ = x
                if b == NB - 1 and not (isinstance(w, int) and w == 2 * NP - 1):
                    next_weights(w + 1)

            def slot(w, b, now, nxt, later):
                low(nxt, 1)
                rotate(later, 0)
                rotate(later, 1)
                low(nxt, 2)
                peak(nxt, 0)
                peak(nxt, 1)
                peak(nxt, 2)
                low(nxt, 3)
                peak(nxt, 3)
                rotate(later, 2)
                for n in turned_in(w, b):
                    norm_split(n, 0)
                peak(nxt, 4)
                rotate(later, 3)
                invert(nxt, 0)
                normalise(nxt, 0)
                normalise(nxt, 1)
                normalise(nxt, 2)
                low_w(later)
                for n in turned_in(w, b):
                    norm_split(n, 1)
                peak(nxt, 5)
                low_o(now)
                low(later, 0)
                peak(nxt, 6)
                peak(nxt, 7)
                add_out(now, 0)
                add_out(now, 1)
                invert(nxt, 1)
                for n in stats_at_end(w, b):
                    norm_stats(n)
                normalise(nxt, 3)
                normalise(nxt, 4)
                normalise(nxt, 5)

            norm_stats(0)
            invert_root(dve, 0)
            next_weights(0)
            modulate(0)
            norm_split(0, 0)
            norm_split(0, 1)
            norm_stats(1)
            modulate(1)
            run_slots(dve, slot)

            def mlp(b):
                for f in range(FT):
                    dve.wait_ge(hid_ready, 8 * b + f + 1)
                    if f >= 4:
                        dve.wait_ge(y_step, 8 * b + f - 3)
                    dve.tensor_copy(hid_hi[:, f % 4, :], hid[:, f % 4, :]).then_inc(hid_rounded, 1)
                    dve.wait_ge(hid_rounded, 8 * b + f + 1)
                    dve.tensor_tensor(hid_lo[:, f % 4, :], hid[:, f % 4, :], hid_hi[:, f % 4, :], ALU.subtract)\
                       .then_inc(hid_split, 1)
                dve.wait_ge(biased, 2 * NB + b + 1)
                dve.wait_ge(y_step, 8 * b + 8)
                rows = x[:, bass.ds(b, 1), :, :].rearrange("p a t d -> p (a t d)")
                dve.tensor_tensor(rows, ps[:, 4:6, :].rearrange("p a n -> p (a n)"), rows, ALU.add)\
                   .then_inc(y_added, 1)

            mlp(0)
            norm_split(LAST, 0)
            norm_split(LAST, 1)
            with dve.Fori(1, NB) as b:
                mlp(b)


def rotation_table():
    import numpy as np
    inv = np.float32(1.0) / np.float32(10000.0) ** (np.arange(0, DH, 2, dtype=np.float32) / np.float32(DH))
    angle = np.arange(N, dtype=np.float32)[:, None] * inv[None, :]
    cos, sin = np.cos(angle), np.sin(angle)
    both = np.stack([np.concatenate([cos, cos], 1), np.concatenate([-sin, sin], 1)])
    both = both.reshape(2, TT, 128, 1, DH).transpose(2, 0, 1, 3, 4)
    factor = np.array([DH ** -0.5] * 2 + [1.0] * 2, np.float32).reshape(1, 1, 1, 4, 1)
    return np.ascontiguousarray(both * factor, np.float32)


def kernel(**inputs):
    import numpy as np
    import concourse.bacc as bacc
    from concourse.bass_utils import run_bass_kernel_spmd

    def get(name):
        return np.asarray(inputs[name if name in inputs else "L0_xcond_" + name])

    def by_rows(a, tiles):
        return a.reshape(tiles, -1, a.shape[-1]).transpose(1, 0, 2)

    def pairs(a, apart):
        a = a.reshape(-1, NP, 2, DH // 2, 2) if apart else a.reshape(-1, NP, 2, 2, DH // 2)
        if apart:
            a = a.transpose(0, 1, 2, 4, 3)
        return a.reshape(-1, NP, 128).transpose(1, 0, 2)

    mid = H * DH
    pack = np.zeros((2 * NP, 128, WPACK), np.float32)
    for first, kind in ((0, "sa"), (NP, "ca")):
        wq, wkv, wo = get(kind + "_wq"), get(kind + "_wkv"), get(kind + "_wo")
        q, k, v = pairs(wq, True), pairs(wkv[:, :mid], True), pairs(wkv[:, mid:], False)
        for p in range(NP):
            if first == 0:
                qkv = by_rows(np.concatenate([q[p], k[p], v[p]], 1), KT)
                pack[p, :, 0:WQKV] = qkv.reshape(128, WQKV)
            else:
                pack[first + p, :, 0:KT * 128] = by_rows(q[p], KT).reshape(128, KT * 128)
                kv = by_rows(np.concatenate([k[p], v[p]], 1), KT)
                pack[first + p, 0:CK, KT * 128:WQKV] = kv.reshape(CK, KT * 256)
            pack[first + p, :, WQKV:WPACK] = wo[p * 128:(p + 1) * 128]
    columns = [get(n).reshape(KT, 128).T for n in
               ("ln1_w", "ln1_b", "g1_b", "b1_b", "ln2_w", "ln2_b", "g2_b", "b2_b")]
    columns.append(get("ff_b1").reshape(FT, 128).T)
    arrays = {
        "x_dram": get("x"),
        "ctx_dram": get("ctx_768"),
        "pack_dram": pack,
        "cond_dram": by_rows(get("cond_1024").T, KT),
        "ada_dram": np.stack([by_rows(get(n), KT) for n in ("g1_w", "b1_w", "g2_w", "b2_w")], 1),
        "cols_dram": np.concatenate(columns, 1),
        "ctxln_dram": np.stack([get(n).reshape(KT, CK).T for n in ("ca_lnc_w", "ca_lnc_b")], 1),
        "rows_dram": np.stack([get(n) for n in ("sa_bo", "ca_bo", "ff_b2")]),
        "w1_dram": by_rows(get("ff_w1"), KT),
        "w2_dram": by_rows(get("ff_w2"), FT),
        "rope_dram": rotation_table(),
    }
    arrays = {n: np.ascontiguousarray(a) for n, a in arrays.items()}
    nc = bacc.Bacc("TRN2", target_bir_lowering=False, num_devices=1)
    args = [nc.dram_tensor(n, a.shape, mybir.dt.from_np(a.dtype), kind="ExternalInput").ap()
            for n, a in arrays.items()]
    out = nc.dram_tensor("out", (NB, N, D), F32, kind="ExternalOutput").ap()
    build(nc, *args, out)
    return run_bass_kernel_spmd(nc, [arrays], core_ids=[0]).results[0]["out"]
```
